# Optimizing a Trainium2 kernel written in Bass

```python
import numpy as np
import jax
import jax.numpy as jnp

def _softmax(x, axis=-1):
    return jax.nn.softmax(x, axis=axis)

def _gelu(x):
    return jax.nn.gelu(x, approximate=True)

def _silu(x):
    return jax.nn.silu(x)

def _sigmoid(x):
    return jax.nn.sigmoid(x)

def _layernorm(x, axis=-1, eps=1e-05):
    m = jnp.mean(x, axis=axis, keepdims=True)
    v = jnp.var(x, axis=axis, keepdims=True)
    return (x - m) / jnp.sqrt(v + eps)

def _scatter_add(tgt, idx, src, axis=0):
    return tgt.at[idx].add(src)

def _segment_sum(src, seg, n):
    return jax.ops.segment_sum(src, seg, n)
kernel_name = 'mk_adj_preln_d1_adj_r2_9de3f3'

def setup_inputs(seed: int=0):
    np.random.seed(seed)
    _w = jnp.asarray

    def _rec_inputs():
        import jax
        import jax.numpy as jnp
        _gk = jax.random.key(seed)
        x = -0.003407 + 1.001 * jax.random.normal(jax.random.fold_in(_gk, 1), (3327, 128), jnp.float32)
        _w = (1.0 + jnp.arange(3327, dtype=jnp.float32)) ** (-0.5)
        _w = _w / _w.mean()
        _pij = jnp.clip(0.00120228 * _w[:, None] * _w[None, :], 0.0, 1.0)
        _a = jax.random.uniform(jax.random.fold_in(_gk, 2), (3327, 3327)) < _pij
        _a = jnp.logical_or(_a, jnp.swapaxes(_a, -1, -2))
        _a = jnp.logical_or(_a, jnp.eye(3327, dtype=bool))
        _af = _a.astype(jnp.float32)
        _af = _af * jax.random.uniform(jax.random.fold_in(_gk, 3), (3327, 3327), jnp.float32, 0.05, 1)
        adj = _af
        return (x, adj)
    x, adj = _rec_inputs()

    def _L0_gnn_setup():
        import jax, jax.numpy as jnp
        import numpy as np
        N = 512
        IN_DIM = 128
        OUT_DIM = 128
        HEADS = 4

        def _gatv2_head(x, A_shape, w1, w2, a, Wlin):
            x1 = x @ w1
            x2 = x @ w2
            E = jax.nn.leaky_relu(x1[:, None, :] + x2[None, :, :], negative_slope=0.01)
            s = E @ a
            s = jnp.tanh(s / 8.0) * 8.0
            s = jnp.exp(s) * A_shape
            s = s / jnp.sum(s, axis=-1, keepdims=True)
            out = s @ x @ Wlin.T
            return jax.nn.leaky_relu(out, negative_slope=0.01)
        key = jax.random.key(seed)
        ks = jax.random.split(key, 7)
        x = jax.random.normal(ks[0], (N, IN_DIM), dtype=jnp.float32)
        A_shape = jax.random.uniform(ks[1], (N, N), dtype=jnp.float32)
        w1 = jax.random.normal(ks[2], (HEADS, IN_DIM, OUT_DIM), dtype=jnp.float32)
        w2 = jax.random.normal(ks[3], (HEADS, IN_DIM, OUT_DIM), dtype=jnp.float32)
        a = jax.random.normal(ks[4], (HEADS, OUT_DIM), dtype=jnp.float32)
        Wlin = jax.random.normal(ks[5], (HEADS, OUT_DIM, IN_DIM), dtype=jnp.float32) * (1.0 / np.sqrt(IN_DIM))
        w = jax.random.normal(ks[6], (OUT_DIM * HEADS, OUT_DIM), dtype=jnp.float32)
        return {'x': x, 'A_shape': A_shape, 'w1': w1, 'w2': w2, 'a': a, 'Wlin': Wlin, 'w': w}
    _L0_gnn_all = _L0_gnn_setup()
    _L0_gnn_in = {k: v for k, v in _L0_gnn_all.items() if k in ('w1', 'w2', 'a', 'Wlin', 'w')}
    del _L0_gnn_all
    return {'x': x, 'adj': adj, 'L0_gnn_w1': _L0_gnn_in['w1'], 'L0_gnn_w2': _L0_gnn_in['w2'], 'L0_gnn_a': _L0_gnn_in['a'], 'L0_gnn_Wlin': _L0_gnn_in['Wlin'], 'L0_gnn_w': _L0_gnn_in['w']}

def reference(x, adj, L0_gnn_w1, L0_gnn_w2, L0_gnn_a, L0_gnn_Wlin, L0_gnn_w):
    import jax
    import jax.numpy as jnp

    def _L0_gnn_ref(x, A_shape, w1, w2, a, Wlin, w):
        import jax, jax.numpy as jnp
        import numpy as np
        N = 512
        IN_DIM = 128
        OUT_DIM = 128
        HEADS = 4

        def _gatv2_head(x, A_shape, w1, w2, a, Wlin):
            x1 = x @ w1
            x2 = x @ w2
            E = jax.nn.leaky_relu(x1[:, None, :] + x2[None, :, :], negative_slope=0.01)
            s = E @ a
            s = jnp.tanh(s / 8.0) * 8.0
            s = jnp.exp(s) * A_shape
            s = s / jnp.sum(s, axis=-1, keepdims=True)
            out = s @ x @ Wlin.T
            return jax.nn.leaky_relu(out, negative_slope=0.01)
        heads = [_gatv2_head(x, A_shape, w1[h], w2[h], a[h], Wlin[h]) for h in range(w1.shape[0])]
        return jnp.concatenate(heads, axis=-1) @ w
    h = jnp.maximum(_layernorm(x, axis=-1), 0.0)
    x = x + _L0_gnn_ref(h, adj, L0_gnn_w1, L0_gnn_w2, L0_gnn_a, L0_gnn_Wlin, L0_gnn_w)
    return x

_drawn_inputs = setup_inputs


def setup_inputs(seed=0):
    import zlib

    import numpy as np

    out = dict(_drawn_inputs(seed))
    spreads = {}
    factors = {}
    for name, (base, spread) in spreads.items():
        noise = np.random.default_rng([zlib.crc32(name.encode()), seed]).standard_normal(out[name].shape)
        drawn = base * np.exp(spread * noise) if base else spread * noise
        out[name] = jnp.asarray(drawn.astype(out[name].dtype))
    for name, factor in factors.items():
        out[name] = (out[name] * factor).astype(out[name].dtype)
    return out
```

```python
import concourse.bass as bass
from concourse import mybir
from contextlib import ExitStack

P = 128


def gatv2_kernel(nc, x, adj, w1, w2, a, wlin, w, out):
    f32, bf16 = mybir.dt.float32, mybir.dt.bfloat16
    u32, i32 = mybir.dt.uint32, mybir.dt.int32
    ALU, ACT, AX = mybir.AluOpType, mybir.ActivationFunctionType, mybir.AxisListType

    N, D = x.shape
    H = w1.shape[0]
    HD = H * D
    NB = (N + P - 1) // P
    LAST = N - P
    SEG = 4
    SW = (N + SEG - 1) // SEG
    NP = SEG * SW
    TOP = 8
    CAND = SEG * TOP
    ROUNDS = CAND // TOP
    REC = 20
    R_COL, R_KEYF, R_KEYU, R_BLK = 8, 16, 17, 18
    FIRST = 1
    CAP = FIRST + NB * P * ROUNDS * (SW // TOP)
    DUMMIES = 3 * P
    FAR = float(1 << 22)
    XW = HD + H
    TW = HD + H + D
    SLOPE = 0.01
    EPS = 1e-5
    assert NB % 2 == 0 and NB <= 32 and SW % TOP == 0 and CAP + DUMMIES < FAR

    x1_dram = nc.dram_tensor("x1_table", (NB * P, XW), f32).ap()
    x2h_dram = nc.dram_tensor("x2h_table", (N, TW), f32).ap()
    list_dram = nc.dram_tensor("unit_list", (CAP + DUMMIES, REC), f32).ap()

    ctx = ExitStack()
    with ctx:
        def sb(name, shape, dt):
            return ctx.enter_context(nc.sbuf_tensor(name, shape, dt))

        def pb(name, shape):
            return ctx.enter_context(nc.psum_tensor(name, shape, f32))

        def sem(name):
            return ctx.enter_context(nc.semaphore(name))

        ident = sb("ident", [P, P], f32)
        before = sb("before", [P, P], bf16)
        ones = sb("ones", [P, P], bf16)
        zeros = sb("zeros", [P, HD], bf16)
        seg_no = sb("seg_no", [P, SEG, TOP], f32)
        thresh = sb("thresh", [P, ROUNDS], f32)
        far4 = sb("far4", [P, ROUNDS], f32)
        k_off = sb("k_off", [P, ROUNDS], f32)
        part_no = sb("part_no", [P, 3], f32)
        row_ids = sb("row_ids", [P, NB * P], f32)
        eps_c = sb("eps_c", [P, 1], f32)
        tiny_c = sb("tiny_c", [P, 1], f32)
        w1_sb = sb("w1_sb", [P, HD], f32)
        w2_sb = sb("w2_sb", [P, HD], f32)
        w1a = sb("w1a", [P, H], f32)
        w2a = sb("w2a", [P, H], f32)
        a_sb = sb("a_sb", [P, HD], f32)
        wlin_sb = sb("wlin_sb", [P, H, P], f32)
        wlinT = sb("wlinT", [P, H, P], f32)
        w_sb = sb("w_sb", [P, H, P], f32)

        adj_t = [sb(f"adj_t{v}", [P, NP], f32) for v in range(2)]
        sign_dump = sb("sign_dump", [P, NP], bf16)
        x_t = [sb(f"x_t{v}", [P, D], f32) for v in range(2)]
        bn6 = sb("bn6", [P, 6], f32)
        mv = sb("mv", [P, 2], f32)
        std = sb("std", [P, 1], f32)
        rstd = sb("rstd", [P, 1], f32)
        shift = sb("shift", [P, 1], f32)
        x1_t = [sb(f"x1_t{v}", [P, XW], f32) for v in range(2)]
        x2h_t = [sb(f"x2h_t{v}", [P, TW], f32) for v in range(2)]
        hT = sb("hT", [P, P], f32)
        counts = [sb(f"counts{v}", [P, 6], f32) for v in range(2)]
        counts_max = [sb(f"counts_max{v}", [P, 6], f32) for v in range(2)]
        m_f = sb("m_f", [1, 1], f32)
        m_i = sb("m_i", [1, 1], i32)
        n_batch = sb("n_batch", [1, 1], i32)
        cum_f = sb("cum_f", [1, 1], f32)
        cum = [sb(f"cum{v}", [1, 2], i32) for v in range(2)]
        c_val = sb("c_val", [P, SEG, TOP], f32)
        c_idx = sb("c_idx", [P, SEG, TOP], u32)
        c_col = sb("c_col", [P, SEG * TOP], f32)
        key = sb("key", [P, CAND], f32)
        keys_left = sb("keys_left", [P, CAND], f32)
        nonzero = sb("nonzero", [P, CAND], f32)
        n_cand = sb("n_cand", [P, 1], f32)
        unit_flag = sb("unit_flag", [P, ROUNDS], f32)
        n_unit = sb("n_unit", [P, 1], f32)
        n_unit16 = sb("n_unit16", [P, 1], bf16)
        top = sb("top", [P, ROUNDS, TOP], f32)
        match = sb("match", [P, CAND, CAND], f32)
        far_top = sb("far_top", [P, CAND], f32)
        rec_out = sb("rec_out", [P, ROUNDS, REC], f32)
        step_f = sb("step_f", [P, ROUNDS], f32)
        step_i = sb("step_i", [P, ROUNDS, 2], i32)
        base = sb("base", [P, 1], f32)
        base_row = sb("base_row", [P, 1], f32)
        far_pos = sb("far_pos", [P, ROUNDS], f32)
        pos = sb("pos", [P, ROUNDS], u32)
        n_list = sb("n_list", [1, 1], i32)
        dummy = sb("filler", [P, REC], f32)
        dummy_pos = sb("filler_pos", [P, 3], u32)

        rec = [sb(f"rec{u}", [P, REC], f32) for u in range(2)]
        ends = [sb(f"ends{u}", [1, 4], i32) for u in range(2)]
        x1_g = [sb(f"x1_g{u}", [P, XW], f32) for u in range(2)]
        g = [sb(f"g{u}", [P, TOP, TW], f32) for u in range(2)]
        score = sb("score", [P, TOP, H], f32)
        linear = sb("linear", [P, TOP, H], f32)
        e_tanh = sb("e_tanh", [P, TOP * H], f32)
        e_exp = sb("e_exp", [P, TOP * H], f32)
        prob = sb("prob", [P, TOP, H], f32)
        diag = sb("diag", [P, TOP * H, P], f32)
        unit_sum = sb("unit_sum", [P, HD + H], f32)
        onehot = sb("onehot", [P, P], f32)
        acc = sb("acc", [P, NB, HD + H], f32)

        den_inv = sb("den_inv", [P, H], f32)
        mean_h = sb("mean_h", [P, HD], f32)
        mean_hT = sb("mean_hT", [P, HD], f32)
        relu_T = sb("relu_T", [P, HD], f32)
        leaky_T = sb("leaky_T", [P, HD], f32)
        y_t = [sb(f"y_t{v}", [P, D], f32) for v in range(2)]

        ps_t = pb("ps_t", [P, 512])
        ps_x1 = pb("ps_x1", [P, 512])
        ps_x2 = pb("ps_x2", [P, 512])
        ps_pos = pb("ps_pos", [P, 512])
        ps_xa = pb("ps_xa", [P, 512])
        ps_unit = pb("ps_unit", [P, 512])
        ps_row = pb("ps_row", [P, 1024])

        s_w = sem("weights_in")
        s_const = sem("constants_set")
        s_token = {e: sem(f"token_{e}") for e in ("sp", "act", "pe", "dve", "pool")}
        s_wlinT_ps = sem("wlinT_in_psum")
        s_wlinT = sem("wlinT_copied")
        s_wa = sem("wa_ready")
        s_adj = [sem(f"adj_in{v}") for v in range(2)]
        s_x = [sem(f"x_in{v}") for v in range(2)]
        s_adj_free = sem("adj_free")
        s_var = sem("variance")
        s_std = sem("std")
        s_norm = sem("norm_factors")
        s_h = sem("h_ready")
        s_hT_ps = sem("hT_in_psum")
        s_hT = sem("hT_copied")
        s_x12 = sem("x1_x2_in_psum")
        s_tab = sem("table_rows_ready")
        s_tab_out = [sem(f"table_rows_out{v}") for v in range(2)]
        s_cnt = sem("counts_ready")
        s_cnt_max = sem("counts_max_ready")
        s_cum = sem("batch_range_ready")
        s_units = sem("unit_counts_ready")
        s_pos_ps = sem("positions_in_psum")
        s_rec_base = sem("record_keys_set")
        s_scatter = sem("scatter_ready")
        s_rec_out = sem("records_out")
        s_rec_left = sem("record_buffers_free")
        s_filler = sem("fillers_out")
        s_dummy = sem("dummy_positions")
        s_list = sem("list_complete")
        s_first = sem("first_record_out")
        s_rec = [sem(f"records_in{u}") for u in range(2)]
        s_rec_free = sem("records_used")
        s_g = [sem(f"rows_gathered{u}") for u in range(2)]
        s_g_free = [sem(f"gathered_rows_used{u}") for u in range(2)]
        s_z = sem("z_ready")
        s_leaky = sem("leaky_ready")
        s_za = sem("leaky_times_a_ready")
        s_score = sem("scores_ready")
        s_exp = sem("exp_ready")
        s_diag = sem("diagonals_ready")
        s_unit_ps = sem("unit_sums_in_psum")
        s_unit = sem("unit_sums_ready")
        s_hot = sem("onehot_ready")
        s_row = sem("row_sums_in_psum")
        s_row_used = sem("row_sums_used")
        s_acc = sem("all_rows_summed")
        s_mean = sem("means_ready")
        s_meanT_ps = sem("meansT_in_psum")
        s_meanT = sem("meansT_copied")
        s_lin_ps = sem("wlin_product_in_psum")
        s_relu = sem("relu_out_ready")
        s_lin = sem("leaky_out_ready")
        s_y_ps = sem("w_product_in_psum")
        s_x3 = [sem(f"x_again_in{v}") for v in range(2)]
        s_y = sem("y_ready")
        s_out = [sem(f"y_out{v}") for v in range(2)]

        SETUP_CONST = 13
        SETUP_W = 6 * 16

        def wait_turn(eng, who, s, value):
            eng.wait_ge(s, value)
            eng.sem_inc(s_token[who])

        def first_row(b):
            is_last = (b + (32 - (NB - 1))) >> 5
            row = b * P - is_last * (NB * P - N)
            return row.with_bounds(min_val=0, max_val=LAST)

        block = ctx.enter_context(nc.Block())

        @block.sync
        def _(sp):
            sp.dma_start(w1_sb[:].rearrange("p (h o) -> p h o", h=H), w1.rearrange("h i o -> i h o")).then_inc(s_w, 16)
            sp.dma_start(w2_sb[:].rearrange("p (h o) -> p h o", h=H), w2.rearrange("h i o -> i h o")).then_inc(s_w, 16)
            sp.dma_start(a_sb[:], a.rearrange("(z h) o -> z (h o)", z=1).to_broadcast((P, HD))).then_inc(s_w, 16)
            sp.dma_start(wlin_sb[:], wlin.rearrange("h o i -> o h i")).then_inc(s_w, 16)
            sp.dma_start(w_sb[:], w.rearrange("(h o) n -> o h n", h=H)).then_inc(s_w, 16)
            sp.wait_ge(s_const, SETUP_CONST)
            sp.dma_start(list_dram[0:1, :], zeros[0:1, 0:2 * REC].bitcast(f32)).then_inc(s_first, 16)
            with sp.Fori(0, NB // 2) as i:
                for v in range(2):
                    b = i * 2 + v
                    wait_turn(sp, "sp", s_adj_free, b + 1)
                    sp.dma_start(adj_t[v][:, 0:N], adj[bass.ds(first_row(b), P), :]).then_inc(s_adj[v], 16)
                    wait_turn(sp, "sp", s_h, b + 1)
                    sp.dma_start(x_t[v][:], x[bass.ds(first_row(b), P), :]).then_inc(s_x[v], 16)

            sp.wait_ge(s_first, 16)
            sp.wait_ge(s_list, 1)
            n_units = sp.value_load(n_list[0:1, 0:1], min_val=0, max_val=CAP)
            n_pairs = sp.snap((n_units + 255) >> 8)

            def load_records(t, u, free):
                if free is not None:
                    wait_turn(sp, "sp", s_rec_free, free)
                sp.dma_start(rec[u][:], list_dram[bass.ds(t * P + FIRST, P), :]).then_inc(s_rec[u], 16)
                sp.dma_start(ends[u][:].bitcast(f32).rearrange("o (e z) -> o e z", z=2),
                             list_dram[bass.ds(t * P + FIRST - 1, 2, P), R_BLK:REC]
                             .rearrange("(o e) z -> o e z", o=1)).then_inc(s_rec[u], 16)

            load_records(0, 0, None)
            with sp.Fori(0, n_pairs) as i:
                load_records(i * 2 + 1, 1, i * 2 + 1)
                load_records(i * 2 + 2, 0, i * 2 + 2)

            with sp.Fori(0, NB // 2) as i:
                for v in range(2):
                    b = i * 2 + v
                    wait_turn(sp, "sp", s_y, i * 2 + v + 1)
                    sp.dma_start(x_t[v][:], x[bass.ds(first_row(b), P), :]).then_inc(s_x3[v], 16)
                    wait_turn(sp, "sp", s_y, i * 2 + v + 3)
                    sp.dma_start(out[bass.ds(first_row(b), P), :], y_t[v][:]).then_inc(s_out[v], 16)
                    wait_turn(sp, "sp", s_out[v], i * 16 + 16)

        @block.gpsimd
        def _(pool):
            def const(ins):
                ins.then_inc(s_const, 1)

            const(pool.memset(ident[:], 0.0))
            const(pool.memset(before[:], 1.0))
            const(pool.memset(ones[:], 1.0))
            const(pool.memset(zeros[:], 0.0))
            pool.wait_ge(s_const, 4)
            const(pool.affine_select(out=ident[:], in_=ident[:], compare_op=ALU.not_equal, fill=1.0, base=0,
                                     pattern=[[-1, P]], channel_multiplier=1))
            const(pool.affine_select(out=before[:], in_=before[:], compare_op=ALU.is_gt, fill=0.0, base=0,
                                     pattern=[[1, P]], channel_multiplier=-1))

            def iota(t, pattern, base=0, mult=0):
                return pool.iota(t, pattern, base=base, channel_multiplier=mult, allow_small_or_imprecise_dtypes=True)

            const(iota(seg_no[:], [[1, SEG], [0, TOP]], base=1))
            const(iota(thresh[:], [[TOP, ROUNDS]]))
            const(iota(k_off[:], [[1, ROUNDS]]))
            const(iota(part_no[:], [[P, 3]], mult=1))
            const(iota(row_ids[:], [[1, NB * P]]))
            const(pool.memset(far4[:], FAR))
            pool.memset(eps_c[:], EPS)
            pool.memset(tiny_c[:], 1.2e-38)
            pool.memset(step_f[:], float(P))
            pool.memset(step_i[:, :, 0], P)
            pool.memset(step_i[:, :, 1], 1)
            pool.memset(dummy[:, 0:TOP], 0.0)
            pool.memset(dummy[:, R_COL:R_KEYF].bitcast(i32), int(FAR))
            pool.memset(dummy[:, R_KEYF:R_KEYU], float(NB * P - 1))
            pool.memset(dummy[:, R_KEYU:R_BLK].bitcast(i32), NB * P - 1)
            pool.memset(dummy[:, R_BLK:R_BLK + 1].bitcast(i32), NB - 1)
            pool.memset(dummy[:, R_BLK + 1:REC], 0.0)
            pool.memset(rec_out[:, :, 0:REC], 0.0)
            pool.drain()
            iota(rec_out[:, :, R_KEYF], [[0, ROUNDS]], base=-P, mult=1)
            iota(rec_out[:, :, R_KEYU].bitcast(i32), [[0, ROUNDS]], base=-P, mult=1)
            pool.memset(rec_out[:, :, R_BLK].bitcast(i32), -1)
            for v in range(2):
                pool.memset(counts[v][:, 5:6], 1.0)
                pool.memset(adj_t[v][:, N:NP], 0.0).then_inc(s_adj_free, 1)
            for u in range(2):
                pool.memset(g[u][:], 0.0).then_inc(s_g_free[u], 1)
            pool.memset(acc[:], 0.0)
            const(pool.drain())

            with pool.Fori(0, NB // 2) as i:
                for v in range(2):
                    b = i * 2 + v
                    wait_turn(pool, "pool", s_cnt, b + 1)
                    pool.partition_all_reduce(counts_max[v][:], counts[v][:], P,
                                              bass.bass_isa.ReduceOp.max).then_inc(s_cnt_max, 1)
                    pool.tensor_tensor(rec_out[:, :, R_KEYF], rec_out[:, :, R_KEYF], step_f[:],
                                       ALU.add).then_inc(s_rec_base, 1)
                    pool.tensor_tensor(rec_out[:, :, R_KEYU:R_BLK + 1].bitcast(i32),
                                       rec_out[:, :, R_KEYU:R_BLK + 1].bitcast(i32), step_i[:], ALU.add).then_inc(s_rec_base, 1)
                    wait_turn(pool, "pool", s_rec_base, b * 2 + 2)
                    wait_turn(pool, "pool", s_cum, b + 1)
                    lo = pool.value_load(cum[v][0:1, 0:1], min_val=0, max_val=NB * P)
                    hi = pool.value_load(cum[v][0:1, 1:2], min_val=1, max_val=NB * P)
                    with pool.Fori(lo, hi) as n:
                        wait_turn(pool, "pool", s_scatter, n + 1)
                        for k in range(ROUNDS):
                            pool.indirect_dma_start(
                                list_dram, bass.IndirectOffsetOnAxis(ap=pos[:, k:k + 1], axis=0),
                                rec_out[:, k, :], None, bounds_check=CAP - 1, oob_is_err=False).then_inc(s_rec_out, 16)
                        wait_turn(pool, "pool", s_rec_out, n * (16 * ROUNDS) + 16 * ROUNDS)
                        pool.sem_inc(s_rec_left, 1)
            pool.wait_ge(s_dummy, 1)
            for j in range(3):
                pool.indirect_dma_start(
                    list_dram, bass.IndirectOffsetOnAxis(ap=dummy_pos[:, j:j + 1], axis=0),
                    dummy[:], None, bounds_check=CAP + DUMMIES - 1, oob_is_err=False).then_inc(s_filler, 16)
            pool.wait_ge(s_filler, 48)
            pool.drain().then_inc(s_list, 1)

            pool.wait_ge(s_tab_out[0], 32 * (NB // 2))
            pool.wait_ge(s_tab_out[1], 32 * (NB // 2 + 1))
            n_units = pool.value_load(n_list[0:1, 0:1], min_val=0, max_val=CAP)
            n_pairs = pool.snap((n_units + 255) >> 8)

            def gather(u, turn):
                wait_turn(pool, "pool", s_rec[u], turn * 32)
                wait_turn(pool, "pool", s_g_free[u], turn)
                pool.indirect_dma_start(x1_g[u][:], None, x1_dram, bass.IndirectOffsetOnAxis(
                    ap=rec[u][:, R_KEYU:R_KEYU + 1].bitcast(u32), axis=0), bounds_check=NB * P - 1,
                    oob_is_err=False).then_inc(s_g[u], 16)
                for s in range(TOP):
                    pool.indirect_dma_start(g[u][:, s, :], None, x2h_dram, bass.IndirectOffsetOnAxis(
                        ap=rec[u][:, R_COL + s:R_COL + s + 1].bitcast(u32), axis=0), bounds_check=N - 1,
                        oob_is_err=False).then_inc(s_g[u], 16)

            def times_a(u, t):
                wait_turn(pool, "pool", s_leaky, t + 1)
                pool.tensor_tensor(g[u][:, :, 0:HD], g[u][:, :, 0:HD],
                                   a_sb[:, None, :].to_broadcast((P, TOP, HD)), ALU.mult).then_inc(s_za, 1)

            gather(0, 1)
            with pool.Fori(0, n_pairs) as i:
                gather(1, i + 1)
                times_a(0, i * 2)
                gather(0, i + 2)
                times_a(1, i * 2 + 1)

        @block.scalar
        def _(act):
            act.wait_ge(s_const, SETUP_CONST)
            act.wait_ge(s_wlinT_ps, 1)
            nc.scalar.activation(wlinT[:].rearrange("p h o -> p (h o)"), ps_x1[:], ACT.Copy).then_inc(s_wlinT, 1)
            act.sem_inc(s_tab_out[1], 32)
            with act.Fori(0, NB // 2) as i:
                for v in range(2):
                    b = i * 2 + v
                    wait_turn(act, "act", s_adj[v], i * 16 + 16)
                    for s in range(SEG):
                        nc.scalar.activation(sign_dump[:, s * SW:(s + 1) * SW], adj_t[v][:, s:NP:SEG], ACT.Sign,
                                             accum_out=counts[v][:, s:s + 1])
                    act.drain()
                    nc.scalar.activation(sign_dump[:], adj_t[v][:], ACT.Sign, bias=tiny_c[:],
                                         accum_out=counts[v][:, 4:5])
                    act.drain()
                    nc.scalar.activation(counts[v][:, 4:5], counts[v][:, 4:5], ACT.Copy, scale=-500.0,
                                         bias=500.0 * NP).then_inc(s_cnt, 1)
                    wait_turn(act, "act", s_var, b + 1)
                    nc.scalar.activation(std[:], mv[:, 1:2], ACT.Sqrt, bias=eps_c[:]).then_inc(s_std, 1)
                    wait_turn(act, "act", s_norm, b + 1)
                    nc.scalar.activation(x2h_t[v][:, XW:TW], x_t[v][:], ACT.Relu, bias=shift[:],
                                         scale=rstd[:]).then_inc(s_h, 1)
                    wait_turn(act, "act", s_hT_ps, b + 1)
                    nc.scalar.activation(hT[:], ps_t[:, 0:P], ACT.Copy).then_inc(s_hT, 1)
                    wait_turn(act, "act", s_x12, b + 1)
                    nc.scalar.activation(x1_t[v][:, 0:HD], ps_x1[:], ACT.Copy)
                    nc.scalar.activation(x1_t[v][:, HD:XW], ps_xa[:, 0:H], ACT.Copy)
                    nc.scalar.activation(x2h_t[v][:, HD:XW], ps_xa[:, H:2 * H], ACT.Copy)
                    nc.scalar.activation(x2h_t[v][:, 0:HD], ps_x2[:], ACT.Copy)
                    act.drain().then_inc(s_tab, 1)
                    wait_turn(act, "act", s_tab, b + 1)
                    wait_turn(act, "act", s_tab_out[1 - v], i * 32 + 32)
                    act.dma_start(x1_dram[bass.ds(b * P, P), :], x1_t[v][:]).then_inc(s_tab_out[v], 16)
                    act.dma_start(x2h_dram[bass.ds(first_row(b), P), :], x2h_t[v][:]).then_inc(s_tab_out[v], 16)

            act.wait_ge(s_list, 1)
            n_units = act.value_load(n_list[0:1, 0:1], min_val=0, max_val=CAP)
            n_pairs = act.snap((n_units + 255) >> 8)

            def leaky(u, t):
                wait_turn(act, "act", s_z, t + 1)
                nc.scalar.activation(g[u][:, :, 0:HD], g[u][:, :, 0:HD], ACT.Relu).then_inc(s_leaky, 1)

            def weights(t):
                wait_turn(act, "act", s_score, t + 1)
                nc.scalar.activation(e_tanh[:], score[:].rearrange("p s h -> p (s h)"), ACT.Tanh, scale=0.125)
                act.drain()
                nc.scalar.activation(e_exp[:], e_tanh[:], ACT.Exp, scale=8.0).then_inc(s_exp, 1)
                wait_turn(act, "act", s_unit_ps, t + 1)
                nc.scalar.activation(unit_sum[:, 0:HD], ps_unit[:], ACT.Copy).then_inc(s_unit, 1)

            leaky(0, 0)
            with act.Fori(0, n_pairs) as i:
                leaky(1, i * 2 + 1)
                weights(i * 2)
                leaky(0, i * 2 + 2)
                weights(i * 2 + 1)

            with act.Fori(0, NB) as b:
                wait_turn(act, "act", s_meanT_ps, b + 1)
                nc.scalar.activation(mean_hT[:], ps_t[:], ACT.Copy).then_inc(s_meanT, 1)
                wait_turn(act, "act", s_lin_ps, b + 1)
                nc.scalar.activation(relu_T[:], ps_x1[:], ACT.Relu, scale=1.0 - SLOPE).then_inc(s_relu, 1)

        @block.tensor
        def _(pe):
            pe.wait_ge(s_const, SETUP_CONST)
            pe.wait_ge(s_w, 5 * 16)
            for h in range(H):
                last = nc.tensor.transpose(ps_x1[:, h * P:(h + 1) * P], wlin_sb[:, h, :], ident[:])
            last.then_inc(s_wlinT_ps, 1)
            pe.wait_ge(s_wlinT, 1)
            pe.wait_ge(s_wa, 1)
            with pe.Fori(0, NB // 2) as i:
                for v in range(2):
                    b = i * 2 + v
                    wait_turn(pe, "pe", s_h, b + 3)
                    nc.tensor.transpose(ps_t[:, 0:P], x2h_t[v][:, XW:TW], ident[:]).then_inc(s_hT_ps, 1)
                    wait_turn(pe, "pe", s_hT, b + 1)
                    nc.tensor.matmul(ps_xa[:, 0:H], hT[:], w1a[:], start=True, stop=True)
                    nc.tensor.matmul(ps_xa[:, H:2 * H], hT[:], w2a[:], start=True, stop=True)
                    nc.tensor.matmul(ps_x1[:], hT[:], w1_sb[:], start=True, stop=True)
                    nc.tensor.matmul(ps_x2[:], hT[:], w2_sb[:], start=True, stop=True).then_inc(s_x12, 1)
                    wait_turn(pe, "pe", s_cum, b + 1)
                    lo = pe.value_load(cum[v][0:1, 0:1], min_val=0, max_val=NB * P)
                    hi = pe.value_load(cum[v][0:1, 1:2], min_val=1, max_val=NB * P)
                    with pe.Fori(lo, hi) as n:
                        wait_turn(pe, "pe", s_units, n + 1)
                        nc.tensor.matmul(ps_pos[:, 0:1], before[:], n_unit16[:], start=True, stop=True)
                        nc.tensor.matmul(ps_pos[:, 1:2], ones[:], n_unit16[:], start=True,
                                         stop=True).then_inc(s_pos_ps, 1)

            pe.wait_ge(s_list, 1)
            n_units = pe.value_load(n_list[0:1, 0:1], min_val=0, max_val=CAP)
            n_pairs = pe.snap((n_units + 255) >> 8)
            with pe.Fori(0, n_pairs) as i:
                for u in range(2):
                    t = i * 2 + u
                    wait_turn(pe, "pe", s_diag, t + 1)
                    wait_turn(pe, "pe", s_unit, t + 1)
                    for s in range(TOP):
                        for h in range(H):
                            last = nc.tensor.matmul(ps_unit[:, h * P:(h + 1) * P], diag[:, s * H + h, :],
                                                    g[u][:, s, XW:TW], start=(s == 0 and h == 0),
                                                    stop=(s == TOP - 1), skip_group_check=True)
                    last.then_inc(s_unit_ps, 1)
                    pe.drain().then_inc(s_g_free[u], 1)
                    lo = pe.value_load(ends[u][0:1, 0:1], min_val=0, max_val=NB - 1)
                    hi = pe.value_load(ends[u][0:1, 2:3], min_val=0, max_val=NB - 1)
                    wait_turn(pe, "pe", s_unit, t + 2)
                    with pe.Fori(lo, hi + 1) as k:
                        wait_turn(pe, "pe", s_row_used, t + k + 1)
                        wait_turn(pe, "pe", s_hot, t + k + 1)
                        nc.tensor.matmul(ps_row[:, 0:HD], onehot[:], unit_sum[:, 0:HD], start=True, stop=True)
                        nc.tensor.matmul(ps_row[:, HD:HD + H], onehot[:], unit_sum[:, HD:HD + H],
                                         start=True, stop=True).then_inc(s_row, 1)

            with pe.Fori(0, NB) as b:
                wait_turn(pe, "pe", s_mean, b + 1)
                for h in range(H):
                    last = nc.tensor.transpose(ps_t[:, h * P:(h + 1) * P], mean_h[:, h * P:(h + 1) * P], ident[:])
                last.then_inc(s_meanT_ps, 1)
                wait_turn(pe, "pe", s_meanT, b + 1)
                for h in range(H):
                    last = nc.tensor.matmul(ps_x1[:, h * P:(h + 1) * P], wlinT[:, h, :],
                                            mean_hT[:, h * P:(h + 1) * P], start=True, stop=True)
                last.then_inc(s_lin_ps, 1)
                wait_turn(pe, "pe", s_lin, b + 1)
                for h in range(H):
                    last = nc.tensor.matmul(ps_x2[:, 0:D], leaky_T[:, h * P:(h + 1) * P], w_sb[:, h, :],
                                            start=(h == 0), stop=(h == H - 1))
                last.then_inc(s_y_ps, 1)

        @block.vector
        def _(dve):
            V = nc.vector
            dve.wait_ge(s_const, SETUP_CONST)
            V.memset(cum_f[:], 0.0)
            V.memset(base[:], float(FIRST))
            V.memset(cum[0][:], 0).then_inc(s_h, 2)
            V.memset(match[:, 0, :], 0.0).then_inc(s_rec_free, 1)
            V.memset(match[:, 1, :], 0.0).then_inc(s_rec_left, 1)
            V.memset(cum[1][:], 0).then_inc(s_y, 2)
            V.memset(prob[:], 0.0).then_inc(s_unit, 1)
            V.memset(onehot[:], 0.0).then_inc(s_row_used, 1)
            dve.drain()
            dve.wait_ge(s_w, 5 * 16)
            for weight, product in ((w1_sb, w1a), (w2_sb, w2a)):
                V.tensor_tensor(mean_h[:], weight[:], a_sb[:], ALU.mult)
                dve.drain()
                V.tensor_reduce(product[:], mean_h[:].rearrange("p (h o) -> p h o", h=H), AX.X, ALU.add)
                dve.drain()
            V.tensor_scalar(a_sb[:], a_sb[:], 1.0 - SLOPE, None, ALU.mult)
            dve.drain().then_inc(s_wa, 1)

            def take_candidates(v):
                for s in range(SEG):
                    V.max(c_val[:, s, :], adj_t[v][:, s:NP:SEG])
                dve.drain()
                for s in range(SEG):
                    V.max_index(c_idx[:, s, :], c_val[:, s, :], adj_t[v][:, s:NP:SEG])
                dve.drain()

            def emit_units(n):
                V.scalar_tensor_tensor(c_col[:], c_idx[:].rearrange("p s e -> p (s e)"), float(SEG),
                                       seg_no[:].rearrange("p s e -> p (s e)"), ALU.mult, ALU.add)
                V.tensor_scalar(nonzero[:], c_val[:].rearrange("p s e -> p (s e)"), 0.0, 0.0, ALU.not_equal,
                                ALU.add, accum_out=n_cand[:])
                dve.drain()
                V.tensor_tensor(key[:], nonzero[:], c_col[:], ALU.mult)
                V.tensor_scalar(unit_flag[:], thresh[:], n_cand[:], 0.0, ALU.is_lt, ALU.add, accum_out=n_unit[:])
                dve.drain()
                V.tensor_copy(n_unit16[:], n_unit[:]).then_inc(s_units, 1)
                V.max(top[:, 0, :], key[:])
                dve.drain()
                V.match_replace(keys_left[:], top[:, 0, :], key[:], 0.0)
                for k in range(1, ROUNDS):
                    dve.drain()
                    V.max(top[:, k, :], keys_left[:])
                    dve.drain()
                    if k < ROUNDS - 1:
                        V.match_replace(keys_left[:], top[:, k, :], keys_left[:], 0.0)
                top_f = top[:].rearrange("p k e -> p (k e)")
                V.tensor_tensor(match[:], top_f[:, :, None].to_broadcast((P, CAND, CAND)),
                                key[:, None, :].to_broadcast((P, CAND, CAND)), ALU.is_equal)
                V.tensor_scalar(far_top[:], top_f, 0.0, FAR, ALU.is_equal, ALU.mult)
                dve.drain()
                V.tensor_tensor(match[:], match[:], c_val[:].rearrange("p (z s) e -> p z (s e)", z=1)
                                .to_broadcast((P, CAND, CAND)), ALU.mult)
                wait_turn(dve, "dve", s_rec_left, n + 1)
                dve.drain()
                V.tensor_reduce(rec_out[:, :, 0:TOP], match[:].rearrange("p (k e) c -> p k e c", k=ROUNDS),
                                AX.X, ALU.add)
                V.scalar_tensor_tensor(rec_out[:, :, R_COL:R_KEYF].bitcast(u32),
                                       far_top[:].rearrange("p (k e) -> p k e", k=ROUNDS), -1.0, top[:],
                                       ALU.add, ALU.add)
                V.scalar_tensor_tensor(far_pos[:], thresh[:], n_cand[:], far4[:], ALU.is_ge, ALU.mult)
                wait_turn(dve, "dve", s_pos_ps, n + 1)
                V.tensor_tensor(base_row[:], base[:], ps_pos[:, 0:1], ALU.add)
                V.tensor_tensor(base[:], base[:], ps_pos[:, 1:2], ALU.add)
                dve.drain()
                V.scalar_tensor_tensor(pos[:], far_pos[:], base_row[:], k_off[:], ALU.add, ALU.add)
                dve.drain().then_inc(s_scatter, 1)

            with dve.Fori(0, NB // 2) as i:
                for v in range(2):
                    b = i * 2 + v
                    wait_turn(dve, "dve", s_x[v], i * 16 + 16)
                    V.bn_stats(bn6[:], x_t[v][:])
                    dve.drain()
                    V.bn_aggr(mv[:], bn6[:])
                    dve.drain().then_inc(s_var, 1)
                    wait_turn(dve, "dve", s_adj[v], i * 16 + 16)
                    take_candidates(v)
                    wait_turn(dve, "dve", s_std, b + 1)
                    V.reciprocal(rstd[:], std[:])
                    wait_turn(dve, "dve", s_cnt_max, b + 1)
                    V.tensor_reduce(m_f[:], counts_max[v][0:1, :], AX.X, ALU.max)
                    dve.drain()
                    V.scalar_tensor_tensor(shift[:], mv[:, 0:1], -1.0, rstd[:], ALU.mult, ALU.mult).then_inc(s_norm, 1)
                    V.tensor_scalar(m_i[:], m_f[:], float(SW), float(TOP - 1), ALU.min, ALU.add)
                    V.tensor_copy(cum[v][:, 0:1], cum_f[:])
                    dve.drain()
                    V.tensor_scalar(n_batch[:], m_i[:], 3, None, ALU.logical_shift_right)
                    dve.drain()
                    V.tensor_tensor(cum_f[:], cum_f[:], n_batch[:], ALU.add)
                    dve.drain()
                    V.tensor_copy(cum[v][:, 1:2], cum_f[:])
                    dve.drain().then_inc(s_cum, 1)
                    lo = dve.value_load(cum[v][0:1, 0:1], min_val=0, max_val=NB * P)
                    hi = dve.value_load(cum[v][0:1, 1:2], min_val=1, max_val=NB * P)
                    emit_units(lo)
                    with dve.If(hi - lo > 1):
                        with dve.Fori(lo + 1, hi) as n:
                            for s in range(SEG):
                                V.match_replace(adj_t[v][:, s:NP:SEG], c_val[:, s, :], adj_t[v][:, s:NP:SEG], 0.0)
                            dve.drain()
                            take_candidates(v)
                            emit_units(n)
                    dve.drain().then_inc(s_adj_free, 1)
            V.tensor_scalar(dummy_pos[:], part_no[:], base[:], None, ALU.add)
            V.tensor_scalar(n_list[:], base[0:1, :], float(-FIRST), None, ALU.add)
            dve.drain().then_inc(s_dummy, 1)

            n_units = dve.value_load(n_list[0:1, 0:1], min_val=0, max_val=CAP)
            n_pairs = dve.snap((n_units + 255) >> 8)

            def add_x1(u, turn):
                wait_turn(dve, "dve", s_g[u], turn * (16 * (TOP + 1)))
                V.tensor_tensor(g[u][:, :, 0:HD], g[u][:, :, 0:HD],
                                x1_g[u][:, None, 0:HD].to_broadcast((P, TOP, HD)), ALU.add).then_inc(s_z, 1)

            def finish(u, t):
                wait_turn(dve, "dve", s_za, t + 1)
                V.tensor_reduce(score[:], g[u][:, :, 0:HD].rearrange("p s (h d) -> p s h d", h=H), AX.X, ALU.add)
                V.tensor_tensor(linear[:], g[u][:, :, HD:XW], x1_g[u][:, None, HD:XW].to_broadcast((P, TOP, H)),
                                ALU.add)
                dve.drain()
                V.scalar_tensor_tensor(score[:], linear[:], SLOPE, score[:], ALU.mult, ALU.add).then_inc(s_score, 1)
                wait_turn(dve, "dve", s_exp, t + 1)
                V.tensor_tensor(prob[:], e_exp[:].rearrange("p (s h) -> p s h", h=H),
                                rec[u][:, 0:TOP, None].to_broadcast((P, TOP, H)), ALU.mult)
                dve.drain()
                V.tensor_tensor(diag[:], ident[:, None, :].to_broadcast((P, TOP * H, P)),
                                prob[:].rearrange("p s h -> p (s h)")[:, :, None].to_broadcast((P, TOP * H, P)),
                                ALU.mult)
                V.tensor_reduce(unit_sum[:, HD:HD + H], prob[:].rearrange("p s h -> p h s"), AX.X, ALU.add)
                dve.drain().then_inc(s_diag, 1)
                lo = dve.value_load(ends[u][0:1, 0:1], min_val=0, max_val=NB - 1)
                hi = dve.value_load(ends[u][0:1, 2:3], min_val=0, max_val=NB - 1)
                with dve.Fori(lo, hi + 1) as k:
                    V.tensor_scalar(onehot[:], row_ids[:, bass.ds(k * P, P)], rec[u][:, R_KEYF:R_KEYF + 1], None,
                                    ALU.is_equal).then_inc(s_hot, 1)
                    wait_turn(dve, "dve", s_row, t + k + 1)
                    V.tensor_tensor(acc[:, k, :], acc[:, k, :], ps_row[:, 0:HD + H], ALU.add).then_inc(s_row_used, 1)
                dve.drain().then_inc(s_rec_free, 1)

            add_x1(0, 1)
            with dve.Fori(0, n_pairs) as i:
                add_x1(1, i + 1)
                finish(0, i * 2)
                add_x1(0, i + 2)
                finish(1, i * 2 + 1)
            dve.drain()

            with dve.Fori(0, NB // 2) as i:
                for v in range(2):
                    b = i * 2 + v
                    V.reciprocal(den_inv[:], acc[:, b, HD:HD + H])
                    dve.drain()
                    V.tensor_tensor(mean_h[:].rearrange("p (h d) -> p h d", h=H),
                                    acc[:, b, 0:HD].rearrange("p (h d) -> p h d", h=H),
                                    den_inv[:, :, None].to_broadcast((P, H, D)), ALU.mult).then_inc(s_mean, 1)
                    wait_turn(dve, "dve", s_relu, b + 1)
                    V.scalar_tensor_tensor(leaky_T[:], ps_x1[:], SLOPE, relu_T[:], ALU.mult,
                                           ALU.add).then_inc(s_lin, 1)
                    wait_turn(dve, "dve", s_x3[v], i * 16 + 16)
                    wait_turn(dve, "dve", s_y_ps, b + 1)
                    V.tensor_tensor(y_t[v][:], ps_x2[:, 0:D], x_t[v][:], ALU.add).then_inc(s_y, 1)


_INS = ["x", "adj", "L0_gnn_w1", "L0_gnn_w2", "L0_gnn_a", "L0_gnn_Wlin", "L0_gnn_w"]


def kernel(**inputs):
    import numpy as _np
    import concourse.bacc as _bacc
    from concourse import mybir as _mybir
    from concourse.bass_utils import run_bass_kernel_spmd as _run

    nc = _bacc.Bacc("TRN2", target_bir_lowering=False, num_devices=1)
    arrays, args = {}, []
    for name in _INS:
        arr = _np.ascontiguousarray(inputs[name])
        arrays[f"in_{name}"] = arr
        args.append(nc.dram_tensor(f"in_{name}", arr.shape, _mybir.dt.from_np(arr.dtype), kind="ExternalInput").ap())
    args.append(nc.dram_tensor("out_0", inputs["x"].shape, _mybir.dt.float32, kind="ExternalOutput").ap())
    gatv2_kernel(nc, *args)
    r = _run(nc, [arrays], core_ids=[0])
    return r.results[0]["out_0"]
```

```python
import concourse.bass as bass
from concourse import mybir
from contextlib import ExitStack

P = 128


def gatv2_kernel(nc, x, adj, w1, w2, a, wlin, w, out):
    f32, bf16 = mybir.dt.float32, mybir.dt.bfloat16
    u32, i32 = mybir.dt.uint32, mybir.dt.int32
    ALU, ACT, AX = mybir.AluOpType, mybir.ActivationFunctionType, mybir.AxisListType

    N, D = x.shape
    H = w1.shape[0]
    HD = H * D
    NB = (N + P - 1) // P
    LAST = N - P
    SEG = 8
    SW = (N + SEG - 1) // SEG
    NP = SEG * SW
    TOP = 8
    CAND = SEG * TOP
    RANKS = CAND // TOP
    PAIR = 2 * TOP
    REC = 20
    R_COL, R_KEYF, R_KEYU, R_BLK = 8, 16, 17, 18
    FIRST = 1
    CAP = FIRST + NB * P * RANKS * (SW // TOP)
    FILLERS = 5
    FAR = float(1 << 22)
    XW = HD + H
    TW = HD + H + D
    SLOPE = 0.01
    EPS = 1e-5
    LO = 4
    assert NB % 2 == 0 and NB <= 32 and SW % TOP == 0 and CAP + FILLERS * P < FAR

    x1_dram = nc.dram_tensor("x1_table", (NB * P, XW), f32).ap()
    x2h_dram = nc.dram_tensor("x2h_table", (N, TW), f32).ap()
    list_dram = nc.dram_tensor("unit_list", (CAP + FILLERS * P, REC), f32).ap()

    ctx = ExitStack()
    with ctx:
        def sb(name, shape, dt):
            return ctx.enter_context(nc.sbuf_tensor(name, shape, dt))

        def pb(name, shape):
            return ctx.enter_context(nc.psum_tensor(name, shape, f32))

        def sem(name):
            return ctx.enter_context(nc.semaphore(name))

        ident = sb("ident", [P, P], f32)
        before = sb("before", [P, P], bf16)
        ones = sb("ones", [P, P], bf16)
        zeros = sb("zeros", [P, HD], bf16)
        seg_no = sb("seg_no", [P, SEG, TOP], f32)
        thresh = sb("thresh", [P, RANKS], f32)
        far8 = sb("far8", [P, RANKS], f32)
        rank_no = sb("rank_no", [P, RANKS], f32)
        part_no = sb("part_no", [P, FILLERS], f32)
        col_no = sb("col_no", [P, P], f32)
        block_row = sb("block_row", [P, NB], f32)
        limits = sb("limits", [1, 2], f32)
        round_up = sb("round_up", [1, 2], f32)
        shifts = sb("shifts", [1, 2], i32)
        eps_c = sb("eps_c", [P, 1], f32)
        tiny_c = sb("tiny_c", [P, 1], f32)
        w1_sb = sb("w1_sb", [P, HD], f32)
        w2_sb = sb("w2_sb", [P, HD], f32)
        w1a = sb("w1a", [P, H], f32)
        w2a = sb("w2a", [P, H], f32)
        a_sb = sb("a_sb", [P, HD], f32)
        wlin_sb = sb("wlin_sb", [P, H, P], f32)
        wlinT = sb("wlinT", [P, H, P], f32)
        w_sb = sb("w_sb", [P, H, P], f32)
        x_all = sb("x_all", [P, NB, D], f32)
        row_sum = sb("row_sum", [P, NB], f32)
        mean = sb("mean", [P, NB], f32)
        var = sb("var", [P, NB], f32)
        std = sb("std", [P, NB], f32)
        rstd = sb("rstd", [P, NB], f32)

        adj_t = [sb(f"adj_t{v}", [P, NP], f32) for v in range(2)]
        x1_t = [sb(f"x1_t{v}", [P, XW], f32) for v in range(2)]
        x2h_t = [sb(f"x2h_t{v}", [P, TW], f32) for v in range(2)]
        hT = sb("hT", [P, P], f32)
        C_NEG, C_ONE, C_ROW, C_SEG = SEG, SEG + 1, SEG + 2, SEG + 3
        counts = [sb(f"counts{v}", [P, SEG + 4], f32) for v in range(2)]
        most = [sb(f"most{v}", [P, SEG + 4], f32) for v in range(2)]
        most_f = sb("most_f", [1, 2], f32)
        most_i = sb("most_i", [1, 2], i32)
        n_loop = sb("n_loop", [1, 2], i32)
        n_pair_f = sb("n_pair_f", [1, 1], f32)
        cum_f = sb("cum_f", [1, 2], f32)
        cum = [sb(f"cum{v}", [1, 8], i32) for v in range(2)]
        c_val = sb("c_val", [P, SEG, TOP], f32)
        c_idx = sb("c_idx", [P, SEG, TOP], u32)
        c_col = sb("c_col", [P, CAND], f32)
        key = sb("key", [P, CAND], f32)
        keys_left = sb("keys_left", [P, CAND], f32)
        nonzero = sb("nonzero", [P, CAND], f32)
        n_cand = sb("n_cand", [P, 1], f32)
        unit_flag = sb("unit_flag", [P, RANKS], f32)
        n_unit = sb("n_unit", [P, 1], f32)
        n_unit16 = sb("n_unit16", [P, 1], bf16)
        top = sb("top", [P, 2, TOP], f32)
        match = sb("match", [P, PAIR, CAND], f32)
        far_top = sb("far_top", [P, 2, TOP], f32)
        rec_out = sb("rec_out", [P, 2, REC], f32)
        step_f = sb("step_f", [P, 2], f32)
        step_i = sb("step_i", [P, 2, 2], i32)
        base = sb("base", [P, 1], f32)
        base_row = sb("base_row", [P, 1], f32)
        far_pos = sb("far_pos", [P, RANKS], f32)
        pos_all = sb("pos_all", [P, RANKS], u32)
        pos = sb("pos", [P, 2], u32)
        n_list = sb("n_list", [1, 1], i32)
        filler = sb("filler", [P, REC], f32)
        filler_pos = sb("filler_pos", [P, FILLERS], u32)

        rec = [sb(f"rec{u}", [P, REC], f32) for u in range(2)]
        adj_w = [sb(f"adj_w{u}", [P, TOP], f32) for u in range(2)]
        row_key = [sb(f"row_key{u}", [P, REC - R_KEYF], f32) for u in range(2)]
        ends = [sb(f"ends{u}", [1, 4], i32) for u in range(2)]
        x1_g = [sb(f"x1_g{u}", [P, XW], f32) for u in range(2)]
        g = [sb(f"g{u}", [P, TOP, TW], f32) for u in range(2)]
        h_g = [sb(f"h_g{u}", [P, TOP, D], f32) for u in range(2)]
        score = sb("score", [P, TOP, H], f32)
        linear = sb("linear", [P, TOP, H], f32)
        e_tanh = sb("e_tanh", [P, TOP * H], f32)
        e_exp = sb("e_exp", [P, TOP * H], f32)
        prob = sb("prob", [P, TOP, H], f32)
        diag = sb("diag", [P, TOP * H, P], f32)
        unit_sum = sb("unit_sum", [P, HD], f32)
        unit_den = [sb(f"unit_den{u}", [P, H], f32) for u in range(2)]
        onehot = sb("onehot", [P, P], f32)
        acc = sb("acc", [P, NB, HD + H], f32)

        x_norm = diag[:, 0:NB, :]
        x_sq = acc[:, :, 0:D]
        sign_dump = g[0][:].rearrange("p s c -> p (s c)")[:, 0:NP]
        den_inv = sb("den_inv", [P, 2, H], f32)
        y_t = sb("y_t", [P, 2, D], f32)
        mean_h = g[0][:].rearrange("p s c -> p (s c)")[:, 0:2 * HD].rearrange("p (v c) -> p v c", v=2)
        mean_hT = g[0][:].rearrange("p s c -> p (s c)")[:, 2 * HD:4 * HD]
        relu_T = g[1][:].rearrange("p s c -> p (s c)")[:, 0:2 * HD]
        leaky_T = g[1][:].rearrange("p s c -> p (s c)")[:, 2 * HD:4 * HD]

        banks = [pb(f"bank{i}", [P, 1024]) for i in range(4)]
        ps_t = banks[0][:, 0:512]
        ps_x1 = banks[0][:, 512:1024]
        ps_x2 = banks[1][:, 0:512]
        ps_xa = banks[1][:, 512:1024]
        ps_pos = banks[2][:, 0:512]
        ps_unit = banks[2][:, 512:1024]
        ps_row = banks[3]

        s_x = sem("x_in")
        s_w = sem("weights_in")
        s_const = sem("constants_set")
        s_token = {e: sem(f"token_{e}") for e in ("sp", "act", "pe", "dve", "pool")}
        s_stat = sem("layernorm_steps")
        s_sq = sem("squares_ready")
        s_var = sem("variance_ready")
        s_std = sem("std_ready")
        s_norm = sem("x_normalised")
        s_wlinT_ps = sem("wlinT_in_psum")
        s_wlinT = sem("wlinT_copied")
        s_wa = sem("wa_ready")
        s_adj = [sem(f"adj_in{v}") for v in range(2)]
        s_adj_free = sem("adj_free")
        s_h = sem("h_ready")
        s_hT_ps = sem("hT_in_psum")
        s_hT = sem("hT_copied")
        s_x12 = sem("x1_x2_in_psum")
        s_tab = sem("table_rows_ready")
        s_tab_out = [sem(f"table_rows_out{v}") for v in range(2)]
        s_cnt = sem("counts_ready")
        s_row_cnt = sem("row_counts_ready")
        s_most = sem("largest_counts_ready")
        s_cum = sem("batch_range_ready")
        s_units = sem("unit_counts_ready")
        s_pos_ps = sem("positions_in_psum")
        s_rec_base = sem("record_keys_set")
        s_scatter = sem("scatter_ready")
        s_rec_out = sem("records_out")
        s_rec_left = sem("record_buffers_free")
        s_filler_pos = sem("filler_positions")
        s_filler = sem("fillers_out")
        s_list = sem("list_complete")
        s_first = sem("first_record_out")
        s_rec = [sem(f"records_in{u}") for u in range(2)]
        s_adj_w = [sem(f"adj_weights_in{u}") for u in range(2)]
        s_keys = [sem(f"row_keys_in{u}") for u in range(2)]
        s_g_lo = [sem(f"first_slots_gathered{u}") for u in range(2)]
        s_g_hi = [sem(f"last_slots_gathered{u}") for u in range(2)]
        s_max_lo = sem("max_of_first_slots")
        s_max_hi = sem("max_of_last_slots")
        s_mul_lo = sem("products_of_first_slots")
        s_score = sem("scores_ready")
        s_exp = sem("exp_ready")
        s_prob = sem("weights_ready")
        s_h_g = sem("h_rows_copied")
        s_diag = sem("diagonals_ready")
        s_unit_ps = sem("unit_sums_in_psum")
        s_unit = sem("unit_sums_copied")
        s_hot = sem("onehot_ready")
        s_row = sem("row_sums_in_psum")
        s_row_used = sem("row_sums_used")
        s_tile = sem("tiles_summed")
        s_mean = sem("means_ready")
        s_meanT_ps = sem("meansT_in_psum")
        s_meanT = sem("meansT_copied")
        s_lin_ps = sem("wlin_product_in_psum")
        s_relu = sem("relu_out_ready")
        s_lin = sem("leaky_out_ready")
        s_y_ps = sem("w_product_in_psum")
        s_y = sem("y_ready")
        s_out = sem("y_out")
        s_y_free = sem("y_left")

        SETUP_CONST = 17
        SETUP_W = 5 * 16

        def wait_turn(eng, who, s, value):
            eng.wait_ge(s, value)
            eng.sem_inc(s_token[who])

        def first_row(b):
            is_last = (b + (32 - (NB - 1))) >> 5
            row = b * P - is_last * (NB * P - N)
            return row.with_bounds(min_val=0, max_val=LAST)

        def tile_pairs(eng):
            n_units = eng.value_load(n_list[0:1, 0:1], min_val=0, max_val=CAP)
            n_tiles = (n_units + (P - 1)) >> 7
            return eng.snap((n_tiles + 3) >> 1)

        block = ctx.enter_context(nc.Block())

        @block.sync
        def _(sp):
            sp.dma_start(x_all[:, 0:NB - 1, :], x[0:(NB - 1) * P, :].rearrange("(b p) d -> p b d", p=P)).then_inc(s_x, 16)
            sp.dma_start(x_all[:, NB - 1, :], x[LAST:N, :]).then_inc(s_x, 16)
            sp.dma_start(w1_sb[:].rearrange("p (h o) -> p h o", h=H), w1.rearrange("h i o -> i h o")).then_inc(s_w, 16)
            sp.dma_start(w2_sb[:].rearrange("p (h o) -> p h o", h=H), w2.rearrange("h i o -> i h o")).then_inc(s_w, 16)
            sp.dma_start(a_sb[:], a.rearrange("(z h) o -> z (h o)", z=1).to_broadcast((P, HD))).then_inc(s_w, 16)
            sp.dma_start(wlin_sb[:], wlin.rearrange("h o i -> o h i")).then_inc(s_w, 16)
            sp.dma_start(w_sb[:], w.rearrange("(h o) n -> o h n", h=H)).then_inc(s_w, 16)
            with sp.Fori(0, NB // 2) as i:
                for v in range(2):
                    wait_turn(sp, "sp", s_adj_free, i * 2 + v + 1)
                    sp.dma_start(adj_t[v][:, 0:N], adj[bass.ds(first_row(i * 2 + v), P), :]).then_inc(s_adj[v], 16)
            sp.wait_ge(s_const, SETUP_CONST)
            sp.dma_start(list_dram[0:1, :], zeros[0:1, 0:2 * REC].bitcast(f32)).then_inc(s_first, 16)
            sp.wait_ge(s_first, 16)

            sp.wait_ge(s_list, 1)
            n_pairs = tile_pairs(sp)
            for u in range(2):
                if u == 1:
                    sp.sem_inc(s_adj_w[u], 16)
                sp.sem_inc(s_keys[u], 32)
            sp.dma_start(rec[0][:], list_dram[FIRST:FIRST + P, :]).then_inc(s_rec[0], 16)
            with sp.Fori(0, n_pairs) as i:
                for u in range(2):
                    t = i * 2 + u
                    wait_turn(sp, "sp", s_max_hi, t + 1)
                    sp.dma_start(rec[1 - u][:], list_dram[bass.ds((t + 1) * P + FIRST, P), :]).then_inc(s_rec[1 - u], 16)
                    wait_turn(sp, "sp", s_prob, t + 1)
                    sp.dma_start(adj_w[u][:], list_dram[bass.ds(t * P + FIRST, P), 0:TOP]).then_inc(s_adj_w[u], 16)
                    wait_turn(sp, "sp", s_tile, t + 1)
                    sp.dma_start(row_key[u][:], list_dram[bass.ds(t * P + FIRST, P), R_KEYF:REC]).then_inc(s_keys[u], 16)
                    sp.dma_start(ends[u][:].bitcast(f32).rearrange("o (e z) -> o e z", z=2),
                                 list_dram[bass.ds(t * P + FIRST - 1, 2, P), R_BLK:REC]
                                 .rearrange("(o e) z -> o e z", o=1)).then_inc(s_keys[u], 16)

            for u in range(2):
                wait_turn(sp, "sp", s_rec[u], n_pairs * 16 + 16 * (1 - u))
                wait_turn(sp, "sp", s_adj_w[u], n_pairs * 16 + 16 * u)
                wait_turn(sp, "sp", s_keys[u], n_pairs * 32 + 32)

            with sp.Fori(0, NB // 2) as i:
                wait_turn(sp, "sp", s_y, i + 1)
                for v in range(2):
                    sp.dma_start(out[bass.ds(first_row(i * 2 + v), P), :], y_t[:, v, :]).then_inc(s_out, 16)
                    wait_turn(sp, "sp", s_out, (i * 2 + v + 1) * 16)
                sp.sem_inc(s_y_free, 1)
            sp.wait_ge(s_out, NB * 16)

        @block.gpsimd
        def _(pool):
            def const(ins):
                ins.then_inc(s_const, 1)

            def iota(t, pattern, base=0, mult=0):
                return pool.iota(t, pattern, base=base, channel_multiplier=mult, allow_small_or_imprecise_dtypes=True)

            const(pool.memset(ident[:], 0.0))
            const(pool.memset(before[:], 1.0))
            const(pool.memset(ones[:], 1.0))
            const(pool.memset(zeros[:], 0.0))
            pool.wait_ge(s_const, 4)
            const(pool.affine_select(out=ident[:], in_=ident[:], compare_op=ALU.not_equal, fill=1.0, base=0,
                                     pattern=[[-1, P]], channel_multiplier=1))
            const(pool.affine_select(out=before[:], in_=before[:], compare_op=ALU.is_gt, fill=0.0, base=0,
                                     pattern=[[1, P]], channel_multiplier=-1))
            const(iota(seg_no[:], [[1, SEG], [0, TOP]], base=1))
            const(iota(thresh[:], [[TOP, RANKS]]))
            const(iota(rank_no[:], [[1, RANKS]]))
            const(iota(part_no[:], [[P, FILLERS]], mult=1))
            const(iota(col_no[:], [[1, P]]))
            const(iota(block_row[:], [[P, NB]]))
            const(iota(limits[:], [[SW - CAND, 2]], base=CAND))
            const(iota(round_up[:], [[TOP - PAIR, 2]], base=PAIR - 1))
            const(iota(shifts[:], [[-1, 2]], base=4))
            const(pool.memset(far8[:], FAR))
            pool.memset(eps_c[:], EPS)
            pool.memset(tiny_c[:], 1.2e-38)
            pool.memset(step_f[:], float(P))
            pool.memset(step_i[:, :, 0], P)
            pool.memset(step_i[:, :, 1], 1)
            pool.memset(rec_out[:, :, 0:R_KEYF], 0.0)
            iota(rec_out[:, :, R_KEYF], [[0, 2]], base=-P, mult=1)
            iota(rec_out[:, :, R_KEYU].bitcast(i32), [[0, 2]], base=-P, mult=1)
            pool.memset(rec_out[:, :, R_BLK].bitcast(i32), -1)
            pool.memset(rec_out[:, :, R_BLK + 1], 0.0)
            for v in range(2):
                pool.memset(counts[v][:], 1.0)
                pool.memset(adj_t[v][:, N:NP], 0.0).then_inc(s_adj_free, 1)
            const(pool.drain())
            pool.memset(filler[:, 0:TOP], 0.0)
            pool.memset(filler[:, R_COL:R_KEYF].bitcast(i32), int(FAR))
            pool.memset(filler[:, R_KEYF:R_KEYU], float(NB * P - 1))
            pool.memset(filler[:, R_KEYU:R_BLK].bitcast(i32), NB * P - 1)
            pool.memset(filler[:, R_BLK:R_BLK + 1].bitcast(i32), NB - 1)
            pool.memset(filler[:, R_BLK + 1:REC], 0.0)
            pool.memset(g[0][:].rearrange("p s c -> p (s c)")[:, NP:TOP * TW], 0.0)
            pool.memset(g[1][:], 0.0)
            pool.memset(h_g[0][:], 0.0)
            pool.memset(h_g[1][:], 0.0)
            pool.memset(e_exp[:], 0.0)
            for u in range(2):
                pool.memset(adj_w[u][:], 0.0)
                pool.memset(row_key[u][:], 0.0)
                pool.memset(ends[u][:], 0)
                pool.memset(unit_den[u][:], 0.0)

            with pool.Fori(0, NB // 2) as i:
                for v in range(2):
                    b = i * 2 + v
                    wait_turn(pool, "pool", s_row_cnt, b + 1)
                    pool.partition_all_reduce(most[v][:], counts[v][:], P,
                                              bass.bass_isa.ReduceOp.max).then_inc(s_most, 1)
                    pool.tensor_tensor(rec_out[:, :, R_KEYF], rec_out[:, :, R_KEYF], step_f[:],
                                       ALU.add).then_inc(s_rec_base, 1)
                    pool.tensor_tensor(rec_out[:, :, R_KEYU:R_BLK + 1].bitcast(i32),
                                       rec_out[:, :, R_KEYU:R_BLK + 1].bitcast(i32), step_i[:],
                                       ALU.add).then_inc(s_rec_base, 1)
                    wait_turn(pool, "pool", s_rec_base, b * 2 + 2)
                    wait_turn(pool, "pool", s_cum, b + 1)
                    lo = pool.value_load(cum[v][0:1, 1:2], min_val=0, max_val=CAP)
                    hi = pool.value_load(cum[v][0:1, 3:4], min_val=1, max_val=CAP)
                    with pool.Fori(lo, hi) as m:
                        wait_turn(pool, "pool", s_scatter, m + 1)
                        for k in range(2):
                            pool.indirect_dma_start(
                                list_dram, bass.IndirectOffsetOnAxis(ap=pos[:, k:k + 1], axis=0),
                                rec_out[:, k, :], None, bounds_check=CAP - 1, oob_is_err=False).then_inc(s_rec_out, 16)
                        wait_turn(pool, "pool", s_rec_out, m * 32 + 32)
                        pool.sem_inc(s_rec_left, 1)
            pool.wait_ge(s_filler_pos, 1)
            for j in range(FILLERS):
                pool.indirect_dma_start(
                    list_dram, bass.IndirectOffsetOnAxis(ap=filler_pos[:, j:j + 1], axis=0),
                    filler[:], None, bounds_check=CAP + FILLERS * P - 1, oob_is_err=False).then_inc(s_filler, 16)
            pool.wait_ge(s_filler, FILLERS * 16)
            pool.drain().then_inc(s_list, 1)

            pool.wait_ge(s_tab_out[0], 32 * (NB // 2))
            pool.wait_ge(s_tab_out[1], 32 * (NB // 2 + 1))
            n_pairs = tile_pairs(pool)

            def gather(u, slots, s):
                for k in slots:
                    pool.indirect_dma_start(g[u][:, k, :], None, x2h_dram, bass.IndirectOffsetOnAxis(
                        ap=rec[u][:, R_COL + k:R_COL + k + 1].bitcast(u32), axis=0), bounds_check=N - 1,
                        oob_is_err=False).then_inc(s, 16)

            def gather_lo(u):
                pool.indirect_dma_start(x1_g[u][:], None, x1_dram, bass.IndirectOffsetOnAxis(
                    ap=rec[u][:, R_KEYU:R_KEYU + 1].bitcast(u32), axis=0), bounds_check=NB * P - 1,
                    oob_is_err=False).then_inc(s_g_lo[u], 16)
                gather(u, range(LO), s_g_lo[u])

            pool.wait_ge(s_rec[0], 16)
            gather_lo(0)
            gather(0, range(LO, TOP), s_g_hi[0])
            with pool.Fori(0, n_pairs) as i:
                for u in range(2):
                    t = i * 2 + u
                    wait_turn(pool, "pool", s_rec[1 - u], (i + 1 + u) * 16)
                    wait_turn(pool, "pool", s_score, t + 1)
                    wait_turn(pool, "pool", s_h_g, t + 1)
                    gather_lo(1 - u)
                    wait_turn(pool, "pool", s_max_lo, t + 1)
                    pool.tensor_tensor(g[u][:, 0:LO, 0:HD], g[u][:, 0:LO, 0:HD],
                                       a_sb[:, None, :].to_broadcast((P, LO, HD)), ALU.mult).then_inc(s_mul_lo, 1)
                    gather(1 - u, range(LO, TOP), s_g_hi[1 - u])

        @block.scalar
        def _(act):
            act.wait_ge(s_const, SETUP_CONST)
            act.wait_ge(s_wlinT_ps, 1)
            nc.scalar.activation(wlinT[:].rearrange("p h o -> p (h o)"), ps_x1, ACT.Copy).then_inc(s_wlinT, 1)
            act.wait_ge(s_stat, 1)
            nc.scalar.activation(x_sq, x_norm, ACT.Square).then_inc(s_sq, 1)
            act.wait_ge(s_var, 1)
            nc.scalar.activation(std[:], var[:], ACT.Sqrt, bias=eps_c[:], scale=1.0 / D).then_inc(s_std, 1)
            act.wait_ge(s_norm, 1)
            act.sem_inc(s_tab_out[1], 32)
            with act.Fori(0, NB // 2) as i:
                for v in range(2):
                    b = i * 2 + v
                    nc.scalar.activation(x2h_t[v][:, XW:TW], x_norm[:, b, :], ACT.Relu).then_inc(s_h, 1)
                    wait_turn(act, "act", s_adj[v], i * 16 + 16)
                    for s in range(SEG):
                        nc.scalar.activation(sign_dump[:, s * SW:(s + 1) * SW], adj_t[v][:, s:NP:SEG], ACT.Sign,
                                             accum_out=counts[v][:, s:s + 1])
                    wait_turn(act, "act", s_hT_ps, b + 1)
                    nc.scalar.activation(hT[:], ps_t[:, 0:P], ACT.Copy).then_inc(s_hT, 1)
                    act.drain()
                    nc.scalar.activation(sign_dump, adj_t[v][:], ACT.Sign, bias=tiny_c[:],
                                         accum_out=counts[v][:, C_NEG:C_NEG + 1])
                    act.drain()
                    nc.scalar.activation(counts[v][:, C_NEG:C_NEG + 1], counts[v][:, C_NEG:C_NEG + 1], ACT.Copy,
                                         scale=-500.0, bias=500.0 * NP).then_inc(s_cnt, 1)
                    wait_turn(act, "act", s_x12, b + 1)
                    nc.scalar.activation(x1_t[v][:, 0:HD], ps_x1, ACT.Copy, scale=-1.0)
                    nc.scalar.activation(x2h_t[v][:, 0:HD], ps_x2, ACT.Copy)
                    nc.scalar.activation(x1_t[v][:, HD:XW], ps_xa[:, 0:H], ACT.Copy)
                    nc.scalar.activation(x2h_t[v][:, HD:XW], ps_xa[:, H:2 * H], ACT.Copy, scale=SLOPE)
                    act.drain().then_inc(s_tab, 1)
                    wait_turn(act, "act", s_tab, b + 1)
                    wait_turn(act, "act", s_tab_out[1 - v], i * 32 + 32)
                    act.dma_start(x1_dram[bass.ds(b * P, P), :], x1_t[v][:]).then_inc(s_tab_out[v], 16)
                    act.dma_start(x2h_dram[bass.ds(first_row(b), P), :], x2h_t[v][:]).then_inc(s_tab_out[v], 16)

            act.wait_ge(s_list, 1)
            n_pairs = tile_pairs(act)
            with act.Fori(0, n_pairs) as i:
                for u in range(2):
                    t = i * 2 + u
                    wait_turn(act, "act", s_unit_ps, t + 1)
                    nc.scalar.activation(unit_sum[:], ps_unit, ACT.Copy).then_inc(s_unit, 1)
                    wait_turn(act, "act", s_g_lo[u], (i + 1) * (16 * (LO + 1)))
                    wait_turn(act, "act", s_g_hi[u], (i + 1) * (16 * (TOP - LO)))
                    nc.scalar.activation(h_g[u][:], g[u][:, :, XW:TW], ACT.Copy).then_inc(s_h_g, 1)
                    wait_turn(act, "act", s_prob, t + 2)
                    for k in range(TOP):
                        for h in range(H):
                            last = nc.scalar.activation(diag[:, k * H + h, :], ident[:], ACT.Copy,
                                                        scale=prob[:, k, h:h + 1])
                        last.then_inc(s_diag, 1)
                    wait_turn(act, "act", s_score, t + 2)
                    nc.scalar.activation(e_tanh[:], score[:].rearrange("p s h -> p (s h)"), ACT.Tanh, scale=0.125)
                    act.drain()
                    nc.scalar.activation(e_exp[:], e_tanh[:], ACT.Exp, scale=8.0).then_inc(s_exp, 1)

            def copy_means(i):
                for v in range(2):
                    wait_turn(act, "act", s_meanT_ps, i * 2 + v + 1)
                    nc.scalar.activation(
                        mean_hT.rearrange("p (h v r) -> p h v r", h=H, v=2)[:, :, v, :],
                        (ps_t if v == 0 else ps_x1).rearrange("p (h r) -> p h r", h=H), ACT.Copy).then_inc(s_meanT, 1)

            def relu(i):
                wait_turn(act, "act", s_lin_ps, i + 1)
                nc.scalar.activation(relu_T, banks[1][:], ACT.Relu, scale=1.0 - SLOPE).then_inc(s_relu, 1)

            copy_means(0)
            with act.Fori(0, NB // 2 - 1) as i:
                relu(i)
                copy_means(i + 1)
            relu(NB // 2 - 1)

        @block.tensor
        def _(pe):
            pe.wait_ge(s_const, SETUP_CONST)
            pe.wait_ge(s_w, SETUP_W)
            for h in range(H):
                last = nc.tensor.transpose(ps_x1[:, h * P:(h + 1) * P], wlin_sb[:, h, :], ident[:])
            last.then_inc(s_wlinT_ps, 1)
            nc.tensor.matmul(ps_unit, zeros[:, 0:P], zeros[:], start=True, stop=True).then_inc(s_unit_ps, 1)
            pe.wait_ge(s_wlinT, 1)
            pe.wait_ge(s_wa, 1)
            with pe.Fori(0, NB // 2) as i:
                for v in range(2):
                    b = i * 2 + v
                    wait_turn(pe, "pe", s_h, b + 1)
                    nc.tensor.transpose(ps_t[:, 0:P], x2h_t[v][:, XW:TW], ident[:]).then_inc(s_hT_ps, 1)
                    wait_turn(pe, "pe", s_hT, b + 1)
                    nc.tensor.matmul(ps_xa[:, 0:H], hT[:], w1a[:], start=True, stop=True)
                    nc.tensor.matmul(ps_xa[:, H:2 * H], hT[:], w2a[:], start=True, stop=True)
                    nc.tensor.matmul(ps_x1, hT[:], w1_sb[:], start=True, stop=True)
                    nc.tensor.matmul(ps_x2, hT[:], w2_sb[:], start=True, stop=True).then_inc(s_x12, 1)
                    wait_turn(pe, "pe", s_cum, b + 1)
                    lo = pe.value_load(cum[v][0:1, 0:1], min_val=0, max_val=CAP)
                    hi = pe.value_load(cum[v][0:1, 2:3], min_val=1, max_val=CAP)
                    with pe.Fori(lo, hi) as n:
                        wait_turn(pe, "pe", s_units, n + 1)
                        nc.tensor.matmul(ps_pos[:, 0:1], before[:], n_unit16[:], start=True, stop=True)
                        nc.tensor.matmul(ps_pos[:, 1:2], ones[:], n_unit16[:], start=True,
                                         stop=True).then_inc(s_pos_ps, 1)

            pe.wait_ge(s_list, 1)
            n_pairs = tile_pairs(pe)

            def to_rows(n):
                wait_turn(pe, "pe", s_row_used, n + 1)
                wait_turn(pe, "pe", s_hot, n + 1)
                nc.tensor.matmul(ps_row[:, 0:HD], onehot[:], unit_sum[:], start=True, stop=True)
                nc.tensor.matmul(ps_row[:, HD:HD + H], onehot[:], unit_den[u][:], start=True,
                                 stop=True).then_inc(s_row, 1)

            with pe.Fori(0, n_pairs) as i:
                for u in range(2):
                    t = i * 2 + u
                    wait_turn(pe, "pe", s_keys[u], i * 32 + 32)
                    lo = pe.value_load(ends[u][0:1, 0:1], min_val=0, max_val=NB - 1)
                    hi = pe.value_load(ends[u][0:1, 2:3], min_val=0, max_val=NB - 1)
                    wait_turn(pe, "pe", s_unit, t + 1)
                    to_rows(t + lo)
                    with pe.If(hi > lo):
                        with pe.Fori(lo + 1, hi + 1) as k:
                            to_rows(t + k)
                    for k in range(TOP):
                        wait_turn(pe, "pe", s_diag, t * TOP + (TOP + k + 1))
                        for h in range(H):
                            last = nc.tensor.matmul(ps_unit[:, h * P:(h + 1) * P], diag[:, k * H + h, :],
                                                    h_g[1 - u][:, k, :], start=(k == 0 and h == 0),
                                                    stop=(k == TOP - 1), skip_group_check=True)
                    last.then_inc(s_unit_ps, 1)

            def means_transposed(i):
                wait_turn(pe, "pe", s_mean, i + 1)
                for v in range(2):
                    for h in range(H):
                        last = nc.tensor.transpose((ps_t if v == 0 else ps_x1)[:, h * P:(h + 1) * P],
                                                   mean_h[:, v, h * P:(h + 1) * P], ident[:])
                    last.then_inc(s_meanT_ps, 1)

            def times_wlin(i):
                wait_turn(pe, "pe", s_meanT, i * 2 + 2)
                for h in range(H):
                    last = nc.tensor.matmul(banks[1][:, 2 * h * P:2 * (h + 1) * P], wlinT[:, h, :],
                                            mean_hT[:, 2 * h * P:2 * (h + 1) * P], start=True, stop=True)
                last.then_inc(s_lin_ps, 1)

            def times_w(i):
                wait_turn(pe, "pe", s_lin, i + 1)
                for v in range(2):
                    for h in range(H):
                        last = nc.tensor.matmul(ps_pos[:, v * P:(v + 1) * P],
                                                leaky_T[:, (2 * h + v) * P:(2 * h + v + 1) * P], w_sb[:, h, :],
                                                start=(h == 0), stop=(h == H - 1))
                last.then_inc(s_y_ps, 1)

            means_transposed(0)
            with pe.Fori(0, NB // 2 - 1) as i:
                times_wlin(i)
                means_transposed(i + 1)
                times_w(i)
            times_wlin(NB // 2 - 1)
            times_w(NB // 2 - 1)

        @block.vector
        def _(dve):
            V = nc.vector
            V.memset(cum[0][:], 0).then_inc(s_rec_left, 1)
            V.memset(cum[1][:], 0).then_inc(s_row_used, 1)
            V.memset(cum_f[:], 0.0).then_inc(s_max_hi, 1)
            V.memset(base[:], float(FIRST)).then_inc(s_prob, 1)
            V.memset(onehot[:], 0.0).then_inc(s_y_free, 1)
            V.memset(prob[:], 0.0).then_inc(s_score, 1)
            V.memset(score[:], 0.0).then_inc(s_h_g, 1)
            V.memset(linear[:], 0.0).then_inc(s_exp, 1)
            V.memset(n_unit[:], 0.0).then_inc(s_diag, TOP)

            dve.wait_ge(s_x, 32)
            V.tensor_reduce(row_sum[:], x_all[:], AX.X, ALU.add)
            dve.drain()
            V.tensor_scalar(mean[:], row_sum[:], 1.0 / D, None, ALU.mult)
            dve.drain()
            V.tensor_tensor(x_norm, x_all[:], mean[:, :, None].to_broadcast((P, NB, D)),
                            ALU.subtract).then_inc(s_stat, 1)
            dve.wait_ge(s_w, SETUP_W)
            V.tensor_tensor(unit_sum[:], w1_sb[:], a_sb[:], ALU.mult)
            dve.drain()
            V.tensor_reduce(w1a[:], unit_sum[:].rearrange("p (h o) -> p h o", h=H), AX.X, ALU.add)
            dve.drain()
            V.tensor_tensor(unit_sum[:], w2_sb[:], a_sb[:], ALU.mult)
            dve.drain()
            V.tensor_reduce(w2a[:], unit_sum[:].rearrange("p (h o) -> p h o", h=H), AX.X, ALU.add)
            V.tensor_scalar(a_sb[:], a_sb[:], 1.0 - SLOPE, None, ALU.mult)
            dve.drain().then_inc(s_wa, 1)
            dve.wait_ge(s_sq, 1)
            V.tensor_reduce(var[:], x_sq, AX.X, ALU.add).then_inc(s_var, 1)
            dve.wait_ge(s_std, 1)
            V.reciprocal(rstd[:], std[:])
            dve.drain()
            V.tensor_tensor(x_norm, x_norm, rstd[:, :, None].to_broadcast((P, NB, D)), ALU.mult).then_inc(s_norm, 1)
            V.memset(acc[:], 0.0)
            dve.drain()
            dve.wait_ge(s_const, SETUP_CONST)

            def search(v, steps=()):
                steps = list(steps)
                for s in range(SEG):
                    V.max(c_val[:, s, :], adj_t[v][:, s:NP:SEG])
                    if steps:
                        dve.drain()
                        steps.pop(0)()
                dve.drain()
                for s in range(SEG):
                    V.max_index(c_idx[:, s, :], c_val[:, s, :], adj_t[v][:, s:NP:SEG])
                    if steps:
                        dve.drain()
                        steps.pop(0)()
                dve.drain()
                assert not steps

            def count_units(n):
                V.scalar_tensor_tensor(c_col[:], c_idx[:].rearrange("p s e -> p (s e)"), float(SEG),
                                       seg_no[:].rearrange("p s e -> p (s e)"), ALU.mult, ALU.add)
                V.tensor_scalar(nonzero[:], c_val[:].rearrange("p s e -> p (s e)"), 0.0, 0.0, ALU.not_equal,
                                ALU.add, accum_out=n_cand[:])
                dve.drain()
                V.tensor_tensor(key[:], nonzero[:], c_col[:], ALU.mult)
                V.tensor_scalar(unit_flag[:], thresh[:], n_cand[:], 0.0, ALU.is_lt, ALU.add, accum_out=n_unit[:])
                V.scalar_tensor_tensor(far_pos[:], thresh[:], n_cand[:], far8[:], ALU.is_ge, ALU.mult)
                dve.drain()
                V.tensor_copy(n_unit16[:], n_unit[:]).then_inc(s_units, 1)

            def record_pair(m, q, n):
                if isinstance(q, int):
                    V.max(top[:, 0, :], key[:])
                    dve.drain()
                    V.match_replace(keys_left[:], top[:, 0, :], key[:], 0.0)
                else:
                    V.match_replace(keys_left[:], top[:, 1, :], keys_left[:], 0.0)
                    dve.drain()
                    V.max(top[:, 0, :], keys_left[:])
                    dve.drain()
                    V.match_replace(keys_left[:], top[:, 0, :], keys_left[:], 0.0)
                dve.drain()
                V.max(top[:, 1, :], keys_left[:])
                dve.drain()
                V.tensor_tensor(match[:], top[:].rearrange("p k e -> p (k e)")[:, :, None].to_broadcast((P, PAIR, CAND)),
                                key[:, None, :].to_broadcast((P, PAIR, CAND)), ALU.is_equal)
                V.tensor_scalar(far_top[:], top[:], 0.0, FAR, ALU.is_equal, ALU.mult)
                dve.drain()
                V.tensor_tensor(match[:], match[:], c_val[:].rearrange("p (z s) e -> p z (s e)", z=1)
                                .to_broadcast((P, PAIR, CAND)), ALU.mult)
                wait_turn(dve, "dve", s_rec_left, m + 1)
                V.scalar_tensor_tensor(rec_out[:, :, R_COL:R_KEYF].bitcast(u32), far_top[:], -1.0, top[:],
                                       ALU.add, ALU.add)
                if isinstance(q, int):
                    wait_turn(dve, "dve", s_pos_ps, n + 1)
                    V.tensor_tensor(base_row[:], base[:], ps_pos[:, 0:1], ALU.add)
                    V.tensor_tensor(base[:], base[:], ps_pos[:, 1:2], ALU.add)
                    dve.drain()
                    V.scalar_tensor_tensor(pos_all[:], far_pos[:], base_row[:], rank_no[:], ALU.add, ALU.add)
                dve.drain()
                V.tensor_reduce(rec_out[:, :, 0:TOP], match[:].rearrange("p (k e) c -> p k e c", k=2), AX.X, ALU.add)
                V.tensor_copy(pos[:], pos_all[:, 0:2] if isinstance(q, int) else pos_all[:, bass.ds(q * 2, 2)])
                dve.drain().then_inc(s_scatter, 1)

            def record_units(n, m, per_batch):
                count_units(n)
                record_pair(m, 0, n)
                with dve.If(per_batch > 1):
                    with dve.Fori(1, per_batch) as q:
                        record_pair(m + q, q, n)

            with dve.Fori(0, NB // 2) as i:
                for v in range(2):
                    b = i * 2 + v
                    wait_turn(dve, "dve", s_cnt, b + 1)
                    V.tensor_reduce(counts[v][:, C_ROW:C_ROW + 1], counts[v][:, 0:C_ONE], AX.X,
                                    ALU.add).then_inc(s_row_cnt, 1)

                    def first():
                        V.tensor_copy(cum[v][:, 0:2], cum_f[:])
                        wait_turn(dve, "dve", s_most, b + 1)
                        V.tensor_reduce(most[v][0:1, C_SEG:C_SEG + 1], most[v][0:1, 0:C_ROW], AX.X, ALU.max)

                    search(v, (
                        lambda: None,
                        first,
                        lambda: V.scalar_tensor_tensor(most_f[:], most[v][0:1, C_ROW:C_SEG + 1], 1.0, limits[:],
                                                       ALU.max, ALU.min),
                        lambda: V.tensor_tensor(most_i[:], most_f[:], round_up[:], ALU.add),
                        lambda: V.tensor_tensor(n_loop[:], most_i[:], shifts[:], ALU.logical_shift_right),
                        lambda: V.tensor_tensor(n_pair_f[:], n_loop[:, 0:1], n_loop[:, 1:2], ALU.mult),
                        lambda: (V.tensor_tensor(cum_f[:, 0:1], cum_f[:, 0:1], n_loop[:, 1:2], ALU.add),
                                 V.tensor_tensor(cum_f[:, 1:2], cum_f[:, 1:2], n_pair_f[:], ALU.add)),
                        lambda: (V.tensor_copy(cum[v][:, 2:4], cum_f[:]),
                                 V.tensor_copy(cum[v][:, 4:5], n_loop[:, 0:1])),
                        lambda: dve.drain().then_inc(s_cum, 1)))
                    lo = dve.value_load(cum[v][0:1, 0:1], min_val=0, max_val=CAP)
                    hi = dve.value_load(cum[v][0:1, 2:3], min_val=1, max_val=CAP)
                    m_lo = dve.value_load(cum[v][0:1, 1:2], min_val=0, max_val=CAP)
                    per_batch = dve.value_load(cum[v][0:1, 4:5], min_val=1, max_val=RANKS // 2)
                    record_units(lo, m_lo, per_batch)
                    with dve.If(hi - lo > 1):
                        with dve.Fori(1, hi - lo) as j:
                            for s in range(SEG):
                                V.match_replace(adj_t[v][:, s:NP:SEG], c_val[:, s, :], adj_t[v][:, s:NP:SEG], 0.0)
                            dve.drain()
                            search(v)
                            record_units(lo + j, dve.snap(m_lo + j * per_batch), per_batch)
                    dve.drain().then_inc(s_adj_free, 1)
            V.tensor_scalar(filler_pos[:], part_no[:], base[:], None, ALU.add)
            V.tensor_scalar(n_list[:], base[0:1, :], float(-FIRST), None, ALU.add)
            dve.drain().then_inc(s_filler_pos, 1)

            dve.wait_ge(s_list, 1)
            n_pairs = tile_pairs(dve)

            def half(u, lo, hi, what):
                z = g[u][:, lo:hi, 0:HD]
                if what == "max":
                    return V.tensor_tensor(z, z, x1_g[u][:, None, 0:HD].to_broadcast((P, hi - lo, HD)), ALU.max)
                if what == "mult":
                    return V.tensor_tensor(z, z, a_sb[:, None, :].to_broadcast((P, hi - lo, HD)), ALU.mult)
                return V.tensor_reduce(score[:, lo:hi, :], z.rearrange("p s (h d) -> p s h d", h=H), AX.X, ALU.add)

            def mark_rows(n, k):
                V.scalar_tensor_tensor(onehot[:], col_no[:], block_row[:, bass.ds(k, 1)],
                                       row_key[u][:, 0:1].to_broadcast((P, P)), ALU.add, ALU.is_equal).then_inc(s_hot, 1)

            def add_rows(n, k):
                wait_turn(dve, "dve", s_row, n + 1)
                V.tensor_tensor(acc[:, k, :], acc[:, k, :], ps_row[:, 0:HD + H], ALU.add).then_inc(s_row_used, 1)

            with dve.Fori(0, n_pairs) as i:
                for u in range(2):
                    t = i * 2 + u
                    wait_turn(dve, "dve", s_g_lo[u], (i + 1) * (16 * (LO + 1)))
                    half(u, 0, LO, "max").then_inc(s_max_lo, 1)
                    wait_turn(dve, "dve", s_exp, t + 1)
                    wait_turn(dve, "dve", s_adj_w[1 - u], (i + 1) * 16)
                    wait_turn(dve, "dve", s_diag, t * TOP + TOP)
                    V.tensor_tensor(prob[:], e_exp[:].rearrange("p (s h) -> p s h", h=H),
                                    adj_w[1 - u][:, :, None].to_broadcast((P, TOP, H)), ALU.mult)
                    dve.drain()
                    V.tensor_reduce(unit_den[1 - u][:], prob[:].rearrange("p s h -> p h s"), AX.X, ALU.add)
                    dve.drain().then_inc(s_prob, 1)
                    wait_turn(dve, "dve", s_keys[u], i * 32 + 32)
                    lo = dve.value_load(ends[u][0:1, 0:1], min_val=0, max_val=NB - 1)
                    hi = dve.value_load(ends[u][0:1, 2:3], min_val=0, max_val=NB - 1)
                    mark_rows(t + lo, lo)
                    wait_turn(dve, "dve", s_g_hi[u], (i + 1) * (16 * (TOP - LO)))
                    half(u, LO, TOP, "max").then_inc(s_max_hi, 1)
                    V.tensor_tensor(linear[:], g[u][:, :, HD:XW], x1_g[u][:, None, HD:XW].to_broadcast((P, TOP, H)),
                                    ALU.add)
                    dve.drain()
                    half(u, LO, TOP, "mult")
                    add_rows(t + lo, lo)
                    with dve.If(hi > lo):
                        with dve.Fori(lo + 1, hi + 1) as k:
                            mark_rows(t + k, k)
                            add_rows(t + k, k)
                    dve.drain().then_inc(s_tile, 1)
                    half(u, LO, TOP, "sum")
                    wait_turn(dve, "dve", s_mul_lo, t + 1)
                    half(u, 0, LO, "sum")
                    dve.drain()
                    V.tensor_tensor(score[:], score[:], linear[:], ALU.add).then_inc(s_score, 1)
            wait_turn(dve, "dve", s_g_lo[0], n_pairs * (16 * (LO + 1)) + 16 * (LO + 1))
            wait_turn(dve, "dve", s_g_hi[0], n_pairs * (16 * (TOP - LO)) + 16 * (TOP - LO))
            dve.drain()

            def means(i):
                pair = acc[:, bass.ds(i * 2, 2), :]
                V.reciprocal(den_inv[:], pair[:, :, HD:HD + H])
                dve.drain()
                for v in range(2):
                    V.tensor_tensor(mean_h[:, v, :].rearrange("p (h d) -> p h d", h=H),
                                    pair[:, v, 0:HD].rearrange("p (h d) -> p h d", h=H),
                                    den_inv[:, v, :, None].to_broadcast((P, H, D)), ALU.mult)
                dve.drain().then_inc(s_mean, 1)

            def leaky(i):
                wait_turn(dve, "dve", s_relu, i + 1)
                V.scalar_tensor_tensor(leaky_T, banks[1][:], SLOPE, relu_T, ALU.mult, ALU.add).then_inc(s_lin, 1)

            def result(i):
                wait_turn(dve, "dve", s_y_free, i + 1)
                wait_turn(dve, "dve", s_y_ps, i + 1)
                V.tensor_tensor(y_t[:], ps_pos[:, 0:2 * D].rearrange("p (v d) -> p v d", v=2),
                                x_all[:, bass.ds(i * 2, 2), :], ALU.add).then_inc(s_y, 1)

            means(0)
            with dve.Fori(0, NB // 2 - 1) as i:
                leaky(i)
                means(i + 1)
                result(i)
            leaky(NB // 2 - 1)
            result(NB // 2 - 1)


_INS = ["x", "adj", "L0_gnn_w1", "L0_gnn_w2", "L0_gnn_a", "L0_gnn_Wlin", "L0_gnn_w"]


def kernel(**inputs):
    import numpy as _np
    import concourse.bacc as _bacc
    from concourse import mybir as _mybir
    from concourse.bass_utils import run_bass_kernel_spmd as _run

    nc = _bacc.Bacc("TRN2", target_bir_lowering=False, num_devices=1)
    arrays, args = {}, []
    for name in _INS:
        arr = _np.ascontiguousarray(inputs[name])
        arrays[f"in_{name}"] = arr
        args.append(nc.dram_tensor(f"in_{name}", arr.shape, _mybir.dt.from_np(arr.dtype), kind="ExternalInput").ap())
    args.append(nc.dram_tensor("out_0", inputs["x"].shape, _mybir.dt.float32, kind="ExternalOutput").ap())
    gatv2_kernel(nc, *args)
    r = _run(nc, [arrays], core_ids=[0])
    return r.results[0]["out_0"]
```

```python
import concourse.bass as bass
from concourse import mybir
from contextlib import ExitStack

P = 128


def gatv2_kernel(nc, x, adj, w1, w2, a, wlin, w, out):
    f32, bf16 = mybir.dt.float32, mybir.dt.bfloat16
    u32, i32 = mybir.dt.uint32, mybir.dt.int32
    ALU, ACT, AX = mybir.AluOpType, mybir.ActivationFunctionType, mybir.AxisListType

    N, D = x.shape
    H = w1.shape[0]
    HD = H * D
    NB = (N + P - 1) // P
    LAST = N - P
    SEG = 8
    SW = (N + SEG - 1) // SEG
    NP = SEG * SW
    TOP = 8
    CAND = SEG * TOP
    RANKS = CAND // TOP
    PAIR = 2 * TOP
    REC = 20
    R_COL, R_KEYF, R_KEYU, R_BLK = 8, 16, 17, 18
    FIRST = P + 1
    CAP = FIRST + NB * P * RANKS * (SW // TOP)
    FILLERS = 6
    FAR = float(1 << 22)
    XW = HD + H
    TW = HD + H + D
    SLOPE = 0.01
    EPS = 1e-5
    TAKEN = -3e38
    ROUND = float(1 << 23)
    COPY_AFTER, RELU_AFTER, W_AFTER = 0, 2, 3
    Z_AFTER, FIRST_AFTER = 3, 3
    LO = 5
    assert NB % 2 == 0 and NB <= 32 and SW % TOP == 0 and CAP + FILLERS * P < FAR

    x1_dram = nc.dram_tensor("x1_table", (NB * P, XW), f32).ap()
    x2h_dram = nc.dram_tensor("x2h_table", (N, TW), f32).ap()
    list_dram = nc.dram_tensor("unit_list", (CAP + (FILLERS + 2) * P, REC), f32).ap()

    ctx = ExitStack()
    with ctx:
        def sb(name, shape, dt):
            return ctx.enter_context(nc.sbuf_tensor(name, shape, dt))

        def pb(name, shape):
            return ctx.enter_context(nc.psum_tensor(name, shape, f32))

        def sem(name):
            return ctx.enter_context(nc.semaphore(name))

        ident = sb("ident", [P, P], f32)
        before = sb("before", [P, P], bf16)
        ones = sb("ones", [P, P], bf16)
        zeros = sb("zeros", [P, HD], bf16)
        seg_no = sb("seg_no", [P, SEG, TOP], f32)
        thresh = sb("thresh", [P, RANKS], f32)
        far8 = sb("far8", [P, RANKS], f32)
        rank_no = sb("rank_no", [P, RANKS], f32)
        col_no = sb("col_no", [P, P], f32)
        block_row = sb("block_row", [P, NB], f32)
        limits = sb("limits", [P, 2], f32)
        per_step = sb("per_step", [1, 2], f32)
        round_up = sb("round_up", [1, 2], f32)
        eps_c = sb("eps_c", [P, 1], f32)
        tiny_c = sb("tiny_c", [P, 1], f32)
        w1_sb = sb("w1_sb", [P, HD], f32)
        w2_sb = sb("w2_sb", [P, HD], f32)
        w1a = sb("w1a", [P, H], f32)
        w2a = sb("w2a", [P, H], f32)
        a_sb = sb("a_sb", [P, HD], f32)
        a_T = sb("a_T", [P, H], f32)
        wlin_sb = sb("wlin_sb", [P, H, P], f32)
        wlinT = sb("wlinT", [P, H, P], f32)
        w_sb = sb("w_sb", [P, H, P], f32)
        x_all = sb("x_all", [P, NB, D], f32)
        row_sum = sb("row_sum", [P, NB], f32)
        mean = sb("mean", [P, NB], f32)
        var = sb("var", [P, NB], f32)
        std = sb("std", [P, NB], f32)
        rstd = sb("rstd", [P, NB], f32)

        adj_t = [sb(f"adj_t{v}", [P, NP], f32) for v in range(2)]
        x1_t = [sb(f"x1_t{v}", [P, XW], f32) for v in range(2)]
        x2h_t = [sb(f"x2h_t{v}", [P, TW], f32) for v in range(2)]
        hT = sb("hT", [P, P], f32)
        C_NEG, C_ROW, C_SEG = SEG, SEG + 1, SEG + 2
        counts = [sb(f"counts{v}", [P, C_SEG + 1], f32) for v in range(2)]
        count_dump = sb("count_dump", [P, C_ROW], f32)
        most = [sb(f"most{v}", [P, 2], f32) for v in range(2)]
        count_max = [sb(f"count_max{v}", [P, 2], f32) for v in range(2)]
        n_steps = [sb(f"n_steps{z}", [1, 2], f32) for z in range(2)]
        B_LO, M_LO, B_HI, M_HI, PER = range(5)
        cum_f = sb("cum_f", [1, 5], f32)
        n_new = sb("n_new", [1, 3], f32)
        cum = [sb(f"cum{v}", [1, 5], i32) for v in range(2)]
        c_val = sb("c_val", [P, SEG, TOP], f32)
        c_idx = sb("c_idx", [P, SEG, TOP], u32)
        c_col = sb("c_col", [P, CAND], f32)
        key = sb("key", [P, CAND], f32)
        keys_left = sb("keys_left", [P, CAND], f32)
        nonzero = sb("nonzero", [P, CAND], f32)
        n_cand = sb("n_cand", [P, 1], f32)
        unit_flag = sb("unit_flag", [P, RANKS], f32)
        n_unit = sb("n_unit", [P, 1], f32)
        n_unit16 = sb("n_unit16", [P, 1], bf16)
        top = sb("top", [P, 2, TOP], f32)
        match = sb("match", [P, PAIR, CAND], f32)
        far_top = sb("far_top", [P, 2, TOP], f32)
        rec_out = sb("rec_out", [P, 2, REC], f32)
        step_f = sb("step_f", [P, 2], f32)
        step_i = sb("step_i", [P, 2, 2], i32)
        base = sb("base", [P, 1], f32)
        base_row = sb("base_row", [P, 1], f32)
        far_pos = sb("far_pos", [P, RANKS], f32)
        pos_all = sb("pos_all", [P, RANKS], u32)
        pos = sb("pos", [P, 2], u32)
        n_list = sb("n_list", [1, 1], i32)
        filler = sb("filler", [P, REC], f32)

        rec = [sb(f"rec{u}", [P, REC], f32) for u in range(2)]
        adj_w = [sb(f"adj_w{u}", [P, TOP], f32) for u in range(2)]
        row_key = [sb(f"row_key{u}", [P, REC - R_KEYF], f32) for u in range(2)]
        ends = [sb(f"ends{u}", [1, 6], i32) for u in range(2)]
        x1_g = [sb(f"x1_g{u}", [P, XW], f32) for u in range(2)]
        g = [sb(f"g{u}", [P, TOP, TW], f32) for u in range(2)]
        h_g = [sb(f"h_g{u}", [P, TOP, D], f32) for u in range(2)]
        score = sb("score", [P, TOP, H], f32)
        linear = sb("linear", [P, TOP, H], f32)
        e_tanh = sb("e_tanh", [P, TOP * H], f32)
        e_exp = sb("e_exp", [P, TOP * H], f32)
        prob = sb("prob", [P, TOP, H], f32)
        diag = sb("diag", [P, TOP * H, P], f32)
        unit_sum = sb("unit_sum", [P, HD], f32)
        unit_den = [sb(f"unit_den{u}", [P, H], f32) for u in range(2)]
        onehot = [sb(f"onehot{z}", [P, P], f32) for z in range(2)]
        acc = sb("acc", [P, NB, HD + H], f32)

        x_norm = diag[:, 0:NB, :]
        x_sq = acc[:, :, 0:D]
        sign_dump = g[0][:].rearrange("p s c -> p (s c)")[:, 0:NP]
        den_inv = sb("den_inv", [P, H], f32)
        y_t = sb("y_t", [P, D], f32)
        mean_h = adj_t[0][:, 0:HD]
        mean_hT = adj_t[0][:, HD:2 * HD]
        relu_T = adj_t[0][:, 2 * HD:3 * HD]
        leaky_T = adj_t[0][:, 3 * HD:4 * HD]
        z_T = adj_t[1][:, 0:HD]

        banks = [pb(f"bank{i}", [P, 1024]) for i in range(4)]
        ps_t = banks[0][:, 0:512]
        ps_x1 = banks[0][:, 512:1024]
        ps_x2 = banks[1][:, 0:512]
        ps_xa = banks[1][:, 512:1024]
        ps_pos = banks[2][:, 0:512]
        ps_unit = banks[2][:, 512:1024]
        ps_row = [banks[3], banks[0]]
        ps_meanT = banks[1][:, 0:HD]
        ps_lin = banks[1][:, HD:2 * HD]
        ps_y = banks[2][:, 0:D]
        ps_zT = ps_meanT
        ps_first = banks[2][:, D:D + H]

        s_x = sem("x_in")
        s_w = sem("weights_in")
        s_const = sem("constants_set")
        s_token = {e: sem(f"token_{e}") for e in ("sp", "act", "pe", "dve", "pool")}
        s_stat = sem("layernorm_steps")
        s_sq = sem("squares_ready")
        s_var = sem("variance_ready")
        s_std = sem("std_ready")
        s_norm = sem("x_normalised")
        s_wlinT_ps = sem("wlinT_in_psum")
        s_wlinT = sem("wlinT_copied")
        s_wa = sem("wa_ready")
        s_adj = [sem(f"adj_in{v}") for v in range(2)]
        s_adj_free = sem("adj_free")
        s_h = sem("h_ready")
        s_hT_ps = sem("hT_in_psum")
        s_hT = sem("hT_copied")
        s_x12 = sem("x1_x2_in_psum")
        s_tab = sem("table_rows_ready")
        s_tab_out = [sem(f"table_rows_out{v}") for v in range(2)]
        s_cnt = sem("counts_ready")
        s_row_cnt = sem("row_maxima_ready")
        s_range = sem("steps_to_batch_range")
        s_cum = sem("batch_range_ready")
        s_units = sem("unit_counts_ready")
        s_pos_ps = sem("positions_in_psum")
        s_rec_base = sem("record_keys_set")
        s_match = sem("matches_ready")
        s_weighed = sem("matches_weighed")
        s_scatter = sem("scatter_ready")
        s_rec_out = sem("records_out")
        s_rec_left = sem("record_buffers_free")
        s_filler_set = sem("filler_set")
        s_n_list = sem("list_length_ready")
        s_filler = sem("fillers_out")
        s_list = sem("list_complete")
        s_rec = [sem(f"records_in{u}") for u in range(2)]
        s_adj_w = [sem(f"adj_weights_in{u}") for u in range(2)]
        s_keys = [sem(f"row_keys_in{u}") for u in range(2)]
        s_g_lo = [sem(f"first_slots_gathered{u}") for u in range(2)]
        s_g_hi = [sem(f"last_slots_gathered{u}") for u in range(2)]
        s_max_lo = sem("max_of_first_slots")
        s_max_hi = sem("max_of_last_slots")
        s_mul_lo = sem("products_of_first_slots")
        s_score = sem("scores_ready")
        s_zT_ps = sem("first_slot_transposed")
        s_zT = sem("first_slot_copied")
        s_first = sem("first_scores_in_psum")
        s_exp = sem("exp_ready")
        s_prob = sem("weights_ready")
        s_h_g = sem("h_rows_copied")
        s_diag = sem("diagonals_ready")
        s_unit_ps = sem("unit_sums_in_psum")
        s_unit = sem("unit_sums_copied")
        s_hot = sem("onehot_ready")
        s_row = sem("row_sums_in_psum")
        s_row_used = sem("row_sums_used")
        s_tile = sem("tiles_summed")
        s_mean = sem("means_ready")
        s_meanT_ps = sem("meansT_in_psum")
        s_meanT = sem("meansT_copied")
        s_lin_ps = sem("wlin_product_in_psum")
        s_relu = sem("relu_out_ready")
        s_lin = sem("leaky_out_ready")
        s_y_ps = sem("w_product_in_psum")
        s_y = sem("y_ready")
        s_out = sem("y_out")

        RANGE_STEPS = 9
        SETUP_CONST = 13
        SETUP_W = 5 * 16

        def wait_turn(eng, who, s, value):
            eng.wait_ge(s, value)
            eng.sem_inc(s_token[who])

        def first_row(b):
            if isinstance(b, int):
                return min(b * P, LAST)
            is_last = (b + (32 - (NB - 1))) >> 5
            row = b * P - is_last * (NB * P - N)
            return row.with_bounds(min_val=0, max_val=LAST)

        def next_block(k):
            return (k + 1).with_bounds(min_val=1, max_val=NB - 1)

        def tile_pairs(eng):
            n_units = eng.value_load(n_list[0:1, 0:1], min_val=0, max_val=CAP)
            n_tiles = (n_units + (P - 1)) >> 7
            return eng.snap((n_tiles + 3) >> 1)

        def load_ends(eng, u, n):
            return [eng.value_load(ends[u][0:1, 2 * z:2 * z + 1], min_val=0, max_val=NB - 1) for z in range(n)]

        def part_of_block(eng, begin, end, step, others=None):
            with eng.If(end > begin):
                if others:
                    with eng.If(end - begin > 1):
                        with eng.Fori(begin, end - 1) as k:
                            others(k, k + 1)
                done = end.with_bounds(min_val=1, max_val=NB - 1)
                if step:
                    step((done - 1).with_bounds(min_val=0, max_val=NB - 2), done)

        def from_then_on(eng, step):
            begin = eng.value_load(ends[0][0:1, 0:1], min_val=0, max_val=NB - 1)
            with eng.Fori(begin, NB) as k:
                step(k, k + 1)

        block = ctx.enter_context(nc.Block())

        @block.sync
        def _(sp):
            sp.dma_start(x_all[:, 0:NB - 1, :], x[0:(NB - 1) * P, :].rearrange("(b p) d -> p b d", p=P)).then_inc(s_x, 16)
            sp.dma_start(x_all[:, NB - 1, :], x[LAST:N, :]).then_inc(s_x, 16)
            sp.dma_start(w1_sb[:].rearrange("p (h o) -> p h o", h=H), w1.rearrange("h i o -> i h o")).then_inc(s_w, 16)
            sp.dma_start(w2_sb[:].rearrange("p (h o) -> p h o", h=H), w2.rearrange("h i o -> i h o")).then_inc(s_w, 16)
            sp.dma_start(a_sb[:], a.rearrange("(z h) o -> z (h o)", z=1).to_broadcast((P, HD))).then_inc(s_w, 16)
            sp.dma_start(wlin_sb[:], wlin.rearrange("h o i -> o h i")).then_inc(s_w, 16)
            sp.dma_start(w_sb[:], w.rearrange("(h o) n -> o h n", h=H)).then_inc(s_w, 16)
            with sp.Fori(0, NB // 2) as i:
                for v in range(2):
                    wait_turn(sp, "sp", s_adj_free, i * 2 + v + 1)
                    sp.dma_start(adj_t[v][:, 0:N], adj[bass.ds(first_row(i * 2 + v), P), :]).then_inc(s_adj[v], 16)

            def store(k, done):
                wait_turn(sp, "sp", s_y, done)
                wait_turn(sp, "sp", s_out, done * 16)
                sp.dma_start(out[bass.ds(first_row(k), P), :], y_t[:]).then_inc(s_out, 16)

            sp.wait_ge(s_filler_set, 1)
            sp.wait_ge(s_n_list, 1)
            n_units = sp.value_load(n_list[0:1, 0:1], min_val=0, max_val=CAP)
            sp.dma_start(list_dram[bass.ds(n_units + FIRST, FILLERS * P), :].rearrange("(p j) r -> p j r", p=P),
                         filler[:, None, :].to_broadcast((P, FILLERS, REC))).then_inc(s_filler, 16)

            sp.wait_ge(s_filler, 16)
            sp.wait_ge(s_list, 1)
            n_pairs = tile_pairs(sp)
            for u in range(2):
                if u == 1:
                    sp.sem_inc(s_adj_w[u], 16)
                sp.sem_inc(s_keys[u], 32)
                sp.dma_start(rec[u][:], list_dram[FIRST + u * P:FIRST + (u + 1) * P, :]).then_inc(s_rec[u], 16)
            sp.sem_inc(s_out, 16)
            with sp.Fori(0, n_pairs) as i:
                for u in range(2):
                    t = i * 2 + u
                    wait_turn(sp, "sp", s_prob, t + 1)
                    sp.dma_start(adj_w[u][:], list_dram[bass.ds(t * P + FIRST, P), 0:TOP]).then_inc(s_adj_w[u], 16)
                    wait_turn(sp, "sp", s_keys[u], i * 32 + 32)
                    begin, end = load_ends(sp, u, 2)
                    part_of_block(sp, begin, end, None, others=store)
                    wait_turn(sp, "sp", s_max_hi, t + 2)
                    sp.dma_start(rec[u][:], list_dram[bass.ds((t + 2) * P + FIRST, P), :]).then_inc(s_rec[u], 16)
                    wait_turn(sp, "sp", s_diag, t * TOP + (TOP + 1))
                    wait_turn(sp, "sp", s_tile, t + 1)
                    sp.dma_start(row_key[u][:], list_dram[bass.ds(t * P + FIRST, P), R_KEYF:REC]).then_inc(s_keys[u], 16)
                    sp.dma_start(ends[u][:].bitcast(f32).rearrange("o (e z) -> o e z", z=2),
                                 list_dram[bass.ds(t * P + (FIRST - 1 - P), 3, P), R_BLK:REC]
                                 .rearrange("(o e) z -> o e z", o=1)).then_inc(s_keys[u], 16)
                    part_of_block(sp, begin, end, store)

            for u in range(2):
                wait_turn(sp, "sp", s_rec[u], n_pairs * 16 + 16)
                wait_turn(sp, "sp", s_adj_w[u], n_pairs * 16 + 16 * u)
                wait_turn(sp, "sp", s_keys[u], n_pairs * 32 + 32)
            from_then_on(sp, store)
            sp.wait_ge(s_out, NB * 16 + 16)

        @block.gpsimd
        def _(pool):
            def const(ins):
                ins.then_inc(s_const, 1)

            def iota(t, pattern, base=0, mult=0):
                return pool.iota(t, pattern, base=base, channel_multiplier=mult, allow_small_or_imprecise_dtypes=True)

            const(pool.memset(ident[:], 0.0))
            const(pool.memset(before[:], 1.0))
            const(pool.memset(ones[:], 1.0))
            const(pool.memset(zeros[:], 0.0))
            pool.wait_ge(s_const, 4)
            const(pool.affine_select(out=ident[:], in_=ident[:], compare_op=ALU.not_equal, fill=1.0, base=0,
                                     pattern=[[-1, P]], channel_multiplier=1))
            const(pool.affine_select(out=before[:], in_=before[:], compare_op=ALU.is_gt, fill=0.0, base=0,
                                     pattern=[[1, P]], channel_multiplier=-1))
            const(iota(seg_no[:], [[1, SEG], [0, TOP]], base=1))
            const(iota(thresh[:], [[TOP, RANKS]]))
            const(iota(rank_no[:], [[1, RANKS]]))
            const(iota(col_no[:], [[1, P]]))
            const(iota(block_row[:], [[P, NB]]))
            for z, (m, most_of) in enumerate(((PAIR, CAND), (TOP, SW))):
                pool.memset(limits[:, z:z + 1], float(most_of))
                pool.memset(per_step[:, z:z + 1], 1.0 / m)
                pool.memset(round_up[:, z:z + 1], (m - 1) / (2.0 * m))
            const(pool.memset(far8[:], FAR))
            pool.memset(eps_c[:], EPS)
            pool.memset(tiny_c[:], 1.2e-38)
            pool.memset(step_f[:], float(P))
            pool.memset(step_i[:, :, 0], P)
            pool.memset(step_i[:, :, 1], 1)
            pool.memset(rec_out[:, :, 0:R_KEYF], 0.0)
            iota(rec_out[:, :, R_KEYF], [[0, 2]], base=-P, mult=1)
            iota(rec_out[:, :, R_KEYU].bitcast(i32), [[0, 2]], base=-P, mult=1)
            pool.memset(rec_out[:, :, R_BLK].bitcast(i32), -1)
            pool.memset(rec_out[:, :, R_BLK + 1], 0.0)
            pool.memset(cum_f[:], 0.0)
            for v in range(2):
                pool.memset(adj_t[v][:, N:NP], 0.0).then_inc(s_adj_free, 1)
            const(pool.drain())
            pool.memset(filler[:, 0:TOP], 0.0)
            pool.memset(filler[:, R_COL:R_KEYF].bitcast(i32), int(FAR))
            pool.memset(filler[:, R_KEYF:R_KEYU], float(NB * P - 1))
            pool.memset(filler[:, R_KEYU:R_BLK].bitcast(i32), NB * P - 1)
            pool.memset(filler[:, R_BLK:R_BLK + 1].bitcast(i32), NB - 1)
            pool.memset(filler[:, R_BLK + 1:REC], 0.0)
            pool.drain().then_inc(s_filler_set, 1)
            pool.memset(g[0][:].rearrange("p s c -> p (s c)")[:, NP:TOP * TW], 0.0)
            pool.memset(g[1][:], 0.0)
            pool.memset(h_g[0][:], 0.0)
            pool.memset(h_g[1][:], 0.0)
            pool.memset(e_exp[:], 0.0)
            for u in range(2):
                pool.memset(adj_w[u][:], 0.0)
                pool.memset(row_key[u][:], 0.0)
                pool.memset(ends[u][:], 0)
                pool.memset(unit_den[u][:], 0.0)

            for z in range(2):
                pool.dma_start(list_dram[z * P:z * P + 1, :], zeros[0:1, 0:2 * REC].bitcast(f32)).then_inc(s_rec_out, 16)

            with pool.Fori(0, NB // 2) as i:
                for v in range(2):
                    b = i * 2 + v
                    wait_turn(pool, "pool", s_row_cnt, b + 1)
                    pool.partition_all_reduce(most[v][:], count_max[v][:], P,
                                              bass.bass_isa.ReduceOp.max).then_inc(s_range, 1)
                    wait_turn(pool, "pool", s_range, b * RANGE_STEPS + 1)
                    pool.tensor_tensor(n_steps[0][:], most[v][0:1, :], per_step[:], ALU.mult).then_inc(s_range, 1)
                    pool.tensor_copy(cum_f[:, B_LO:M_LO + 1], cum_f[:, B_HI:M_HI + 1]).then_inc(s_range, 1)
                    wait_turn(pool, "pool", s_range, b * RANGE_STEPS + 3)
                    pool.tensor_tensor(n_steps[1][:], n_steps[0][:], round_up[:], ALU.add).then_inc(s_range, 1)
                    wait_turn(pool, "pool", s_range, b * RANGE_STEPS + 4)
                    pool.tensor_scalar(n_steps[0][:], n_steps[1][:], ROUND, None, ALU.add).then_inc(s_range, 1)
                    wait_turn(pool, "pool", s_range, b * RANGE_STEPS + 5)
                    pool.tensor_scalar(n_new[:, 0:2], n_steps[0][:], -ROUND, None, ALU.add).then_inc(s_range, 1)
                    wait_turn(pool, "pool", s_range, b * RANGE_STEPS + 6)
                    pool.tensor_tensor(n_new[:, 2:3], n_new[:, 0:1], n_new[:, 1:2], ALU.mult).then_inc(s_range, 1)
                    pool.tensor_copy(cum_f[:, PER:PER + 1], n_new[:, 0:1]).then_inc(s_range, 1)
                    wait_turn(pool, "pool", s_range, b * RANGE_STEPS + 8)
                    pool.tensor_tensor(cum_f[:, B_HI:M_HI + 1], cum_f[:, B_LO:M_LO + 1], n_new[:, 1:3],
                                       ALU.add).then_inc(s_range, 1)
                    wait_turn(pool, "pool", s_range, b * RANGE_STEPS + RANGE_STEPS)
                    pool.tensor_copy(cum[v][:], cum_f[:]).then_inc(s_cum, 1)
                    no_sum = zeros[:, 0:2].bitcast(f32).to_broadcast((P, HD + H))
                    pool.tensor_tensor(acc[:, bass.ds(b, 1), :].rearrange("p z c -> p (z c)"), no_sum, no_sum, ALU.add)
                    wait_turn(pool, "pool", s_cum, b + 1)
                    lo = pool.value_load(cum[v][0:1, M_LO:M_LO + 1], min_val=0, max_val=CAP)
                    hi = pool.value_load(cum[v][0:1, M_HI:M_HI + 1], min_val=1, max_val=CAP)
                    wait_turn(pool, "pool", s_rec_out, lo * 32 + 32)
                    pool.tensor_tensor(rec_out[:, :, R_KEYF], rec_out[:, :, R_KEYF], step_f[:],
                                       ALU.add).then_inc(s_rec_base, 1)
                    pool.tensor_tensor(rec_out[:, :, R_KEYU:R_BLK + 1].bitcast(i32),
                                       rec_out[:, :, R_KEYU:R_BLK + 1].bitcast(i32), step_i[:],
                                       ALU.add).then_inc(s_rec_base, 1)
                    wait_turn(pool, "pool", s_rec_base, b * 2 + 2)
                    with pool.Fori(lo, hi) as m:
                        wait_turn(pool, "pool", s_rec_out, m * 32 + 32)
                        pool.sem_inc(s_rec_left, 1)
                        wait_turn(pool, "pool", s_match, m + 1)
                        pool.tensor_tensor(match[:, 0:TOP, :], match[:, 0:TOP, :],
                                           c_val[:].rearrange("p (z s) e -> p z (s e)", z=1)
                                           .to_broadcast((P, TOP, CAND)), ALU.mult).then_inc(s_weighed, 1)
                        wait_turn(pool, "pool", s_scatter, m + 1)
                        for k in range(2):
                            pool.indirect_dma_start(
                                list_dram, bass.IndirectOffsetOnAxis(ap=pos[:, k:k + 1], axis=0),
                                rec_out[:, k, :], None, bounds_check=CAP - 1, oob_is_err=False).then_inc(s_rec_out, 16)
            n_pairs_out = pool.value_load(cum[1][0:1, M_HI:M_HI + 1], min_val=1, max_val=CAP)
            wait_turn(pool, "pool", s_rec_out, n_pairs_out * 32 + 32)
            pool.wait_ge(s_n_list, 1)
            pool.drain().then_inc(s_list, 1)

            pool.wait_ge(s_tab_out[0], 32 * (NB // 2))
            pool.wait_ge(s_tab_out[1], 32 * (NB // 2 + 1))
            n_pairs = tile_pairs(pool)

            def gather(u, slots, s):
                for k in slots:
                    pool.indirect_dma_start(g[u][:, k, :], None, x2h_dram, bass.IndirectOffsetOnAxis(
                        ap=rec[u][:, R_COL + k:R_COL + k + 1].bitcast(u32), axis=0), bounds_check=N - 1,
                        oob_is_err=False).then_inc(s, 16)

            def gather_lo(u):
                pool.indirect_dma_start(x1_g[u][:], None, x1_dram, bass.IndirectOffsetOnAxis(
                    ap=rec[u][:, R_KEYU:R_KEYU + 1].bitcast(u32), axis=0), bounds_check=NB * P - 1,
                    oob_is_err=False).then_inc(s_g_lo[u], 16)
                gather(u, range(LO), s_g_lo[u])

            pool.wait_ge(s_rec[0], 16)
            gather_lo(0)
            gather(0, range(LO, TOP), s_g_hi[0])
            with pool.Fori(0, n_pairs) as i:
                for u in range(2):
                    t = i * 2 + u
                    wait_turn(pool, "pool", s_rec[1 - u], (i + 1 + u) * 16)
                    wait_turn(pool, "pool", s_score, t + 1)
                    wait_turn(pool, "pool", s_h_g, t + 1)
                    gather_lo(1 - u)
                    wait_turn(pool, "pool", s_max_lo, t + 1)
                    pool.tensor_tensor(g[u][:, 1:LO, 0:HD], g[u][:, 1:LO, 0:HD],
                                       a_sb[:, None, :].to_broadcast((P, LO - 1, HD)), ALU.mult).then_inc(s_mul_lo, 1)
                    gather(1 - u, range(LO, TOP), s_g_hi[1 - u])

        @block.scalar
        def _(act):
            act.wait_ge(s_const, SETUP_CONST)
            act.wait_ge(s_wlinT_ps, 1)
            nc.scalar.activation(wlinT[:].rearrange("p h o -> p (h o)"), ps_x1, ACT.Copy).then_inc(s_wlinT, 1)
            act.wait_ge(s_stat, 1)
            nc.scalar.activation(x_sq, x_norm, ACT.Square).then_inc(s_sq, 1)

            def negatives(v):
                nc.scalar.activation(sign_dump, adj_t[v][:], ACT.Sign, bias=tiny_c[:],
                                     accum_out=counts[v][:, C_NEG:C_NEG + 1])
                act.drain()
                nc.scalar.activation(counts[v][:, C_NEG:C_NEG + 1], counts[v][:, C_NEG:C_NEG + 1], ACT.Copy,
                                     scale=-500.0, bias=500.0 * NP)

            def entries(v):
                for s in range(SEG):
                    nc.scalar.activation(sign_dump[:, s * SW:(s + 1) * SW], adj_t[v][:, s:NP:SEG], ACT.Sign,
                                         accum_out=counts[v][:, s:s + 1])
                act.drain()
                nc.scalar.activation(count_dump[:], counts[v][:, 0:C_ROW], ACT.Copy,
                                     accum_out=counts[v][:, C_ROW:C_ROW + 1])
                act.drain().then_inc(s_cnt, 1)

            def h_rows(b, v):
                nc.scalar.activation(x2h_t[v][:, XW:TW], x_norm[:, b, :], ACT.Relu).then_inc(s_h, 1)

            act.wait_ge(s_adj[0], 16)
            negatives(0)
            act.wait_ge(s_var, 1)
            nc.scalar.activation(std[:], var[:], ACT.Sqrt, bias=eps_c[:], scale=1.0 / D).then_inc(s_std, 1)
            act.wait_ge(s_norm, 1)
            h_rows(0, 0)
            entries(0)
            act.sem_inc(s_tab_out[1], 32)

            def table_rows(i, v, last=False):
                b = i * 2 + v
                wait_turn(act, "act", s_hT_ps, b + 1)
                nc.scalar.activation(hT[:], ps_t[:, 0:P], ACT.Copy).then_inc(s_hT, 1)
                wait_turn(act, "act", s_tab_out[1 - v], i * 32 + 32)
                if not last:
                    h_rows(b + 1, 1 - v)
                    wait_turn(act, "act", s_adj[1 - v], (i + v) * 16 + 16)
                    negatives(1 - v)
                    entries(1 - v)
                wait_turn(act, "act", s_x12, b + 1)
                nc.scalar.activation(x1_t[v][:, 0:HD], ps_x1, ACT.Copy, scale=-1.0)
                nc.scalar.activation(x2h_t[v][:, 0:HD], ps_x2, ACT.Copy)
                nc.scalar.activation(x1_t[v][:, HD:XW], ps_xa[:, 0:H], ACT.Copy)
                nc.scalar.activation(x2h_t[v][:, HD:XW], ps_xa[:, H:2 * H], ACT.Copy, scale=SLOPE)
                act.drain().then_inc(s_tab, 1)
                wait_turn(act, "act", s_tab, b + 1)
                act.dma_start(x1_dram[bass.ds(b * P, P), :], x1_t[v][:]).then_inc(s_tab_out[v], 16)
                act.dma_start(x2h_dram[bass.ds(first_row(b), P), :], x2h_t[v][:]).then_inc(s_tab_out[v], 16)

            with act.Fori(0, NB // 2 - 1) as i:
                for v in range(2):
                    table_rows(i, v)
            table_rows(NB // 2 - 1, 0)
            table_rows(NB // 2 - 1, 1, last=True)

            def copy_mean(k, done):
                wait_turn(act, "act", s_meanT_ps, done)
                nc.scalar.activation(mean_hT, ps_meanT, ACT.Copy).then_inc(s_meanT, 1)

            def relu(k, done):
                wait_turn(act, "act", s_lin_ps, done)
                nc.scalar.activation(relu_T, ps_lin, ACT.Relu, scale=1.0 - SLOPE).then_inc(s_relu, 1)

            act.wait_ge(s_list, 1)
            n_pairs = tile_pairs(act)
            nc.scalar.activation(e_tanh[:], zeros[:, 0:2 * TOP * H].bitcast(f32), ACT.Tanh)
            act.drain()
            nc.scalar.activation(e_tanh[:], zeros[:, 0:2 * TOP * H].bitcast(f32), ACT.Exp)
            act.drain()
            with act.Fori(0, n_pairs) as i:
                for u in range(2):
                    t = i * 2 + u
                    wait_turn(act, "act", s_unit_ps, t + 1)
                    nc.scalar.activation(unit_sum[:], ps_unit, ACT.Copy).then_inc(s_unit, 1)
                    wait_turn(act, "act", s_g_lo[u], (i + 1) * (16 * (LO + 1)))
                    wait_turn(act, "act", s_g_hi[u], (i + 1) * (16 * (TOP - LO)))
                    nc.scalar.activation(h_g[u][:], g[u][:, :, XW:TW], ACT.Copy).then_inc(s_h_g, 1)
                    wait_turn(act, "act", s_keys[u], i * 32 + 32)
                    begin, end = load_ends(act, u, 2)
                    part_of_block(act, begin, end, None, others=lambda k, done: (copy_mean(k, done), relu(k, done)))
                    wait_turn(act, "act", s_prob, t + 2)
                    for k in range(TOP):
                        for h in range(H):
                            last = nc.scalar.activation(diag[:, k * H + h, :], ident[:], ACT.Copy,
                                                        scale=prob[:, k, h:h + 1])
                        last.then_inc(s_diag, 1)
                        if k == COPY_AFTER:
                            part_of_block(act, begin, end, copy_mean)
                        if k == Z_AFTER:
                            wait_turn(act, "act", s_zT_ps, t + 1)
                            nc.scalar.activation(z_T, ps_zT, ACT.Copy).then_inc(s_zT, 1)
                        if k == RELU_AFTER:
                            part_of_block(act, begin, end, relu)
                    wait_turn(act, "act", s_score, t + 2)
                    nc.scalar.activation(e_tanh[:], score[:].rearrange("p s h -> p (s h)"), ACT.Tanh, scale=0.125)
                    act.drain()
                    nc.scalar.activation(e_exp[:], e_tanh[:], ACT.Exp, scale=8.0).then_inc(s_exp, 1)
            wait_turn(act, "act", s_keys[0], n_pairs * 32 + 32)
            from_then_on(act, lambda k, done: (copy_mean(k, done), relu(k, done)))

        @block.tensor
        def _(pe):
            pe.wait_ge(s_const, SETUP_CONST)
            pe.wait_ge(s_w, SETUP_W)
            for h in range(H):
                last = nc.tensor.transpose(ps_x1[:, h * P:(h + 1) * P], wlin_sb[:, h, :], ident[:])
            last.then_inc(s_wlinT_ps, 1)
            nc.tensor.matmul(ps_unit, zeros[:, 0:P], zeros[:], start=True, stop=True).then_inc(s_unit_ps, 1)
            pe.wait_ge(s_wlinT, 1)
            pe.wait_ge(s_wa, 1)
            with pe.Fori(0, NB // 2) as i:
                for v in range(2):
                    b = i * 2 + v
                    wait_turn(pe, "pe", s_h, b + 1)
                    nc.tensor.transpose(ps_t[:, 0:P], x2h_t[v][:, XW:TW], ident[:]).then_inc(s_hT_ps, 1)
                    wait_turn(pe, "pe", s_hT, b + 1)
                    nc.tensor.matmul(ps_xa[:, 0:H], hT[:], w1a[:], start=True, stop=True)
                    nc.tensor.matmul(ps_xa[:, H:2 * H], hT[:], w2a[:], start=True, stop=True)
                    nc.tensor.matmul(ps_x1, hT[:], w1_sb[:], start=True, stop=True)
                    nc.tensor.matmul(ps_x2, hT[:], w2_sb[:], start=True, stop=True).then_inc(s_x12, 1)
                    wait_turn(pe, "pe", s_cum, b + 1)
                    lo = pe.value_load(cum[v][0:1, B_LO:B_LO + 1], min_val=0, max_val=CAP)
                    hi = pe.value_load(cum[v][0:1, B_HI:B_HI + 1], min_val=1, max_val=CAP)
                    with pe.Fori(lo, hi) as n:
                        wait_turn(pe, "pe", s_units, n + 1)
                        nc.tensor.matmul(ps_pos[:, 0:1], before[:], n_unit16[:], start=True, stop=True)
                        nc.tensor.matmul(ps_pos[:, 1:2], ones[:], n_unit16[:], start=True,
                                         stop=True).then_inc(s_pos_ps, 1)

            pe.wait_ge(s_list, 1)
            n_pairs = tile_pairs(pe)

            def to_rows(n, z=0):
                if z == 0:
                    wait_turn(pe, "pe", s_row_used, n + 1)
                wait_turn(pe, "pe", s_hot, n + 1)
                nc.tensor.matmul(ps_row[z][:, 0:HD], onehot[z][:], unit_sum[:], start=True, stop=True)
                nc.tensor.matmul(ps_row[z][:, HD:HD + H], onehot[z][:], unit_den[u][:], start=True,
                                 stop=True).then_inc(s_row, 1)

            def mean_transposed(k, done):
                wait_turn(pe, "pe", s_mean, done)
                for h in range(H):
                    last = nc.tensor.transpose(ps_meanT[:, h * P:(h + 1) * P], mean_h[:, h * P:(h + 1) * P], ident[:])
                last.then_inc(s_meanT_ps, 1)

            def times_wlin(k, done):
                wait_turn(pe, "pe", s_meanT, done)
                for h in range(H):
                    last = nc.tensor.matmul(ps_lin[:, h * P:(h + 1) * P], wlinT[:, h, :],
                                            mean_hT[:, h * P:(h + 1) * P], start=True, stop=True)
                last.then_inc(s_lin_ps, 1)

            def times_w(k, done):
                wait_turn(pe, "pe", s_lin, done)
                for h in range(H):
                    last = nc.tensor.matmul(ps_y, leaky_T[:, h * P:(h + 1) * P], w_sb[:, h, :],
                                            start=(h == 0), stop=(h == H - 1))
                last.then_inc(s_y_ps, 1)

            def whole_block(k, done):
                mean_transposed(k, done)
                times_wlin(k, done)
                times_w(k, done)

            with pe.Fori(0, n_pairs) as i:
                for u in range(2):
                    t = i * 2 + u
                    wait_turn(pe, "pe", s_keys[u], i * 32 + 32)
                    begin, lo, hi = load_ends(pe, u, 3)
                    part_of_block(pe, begin, lo, mean_transposed, others=whole_block)
                    wait_turn(pe, "pe", s_unit, t + 1)
                    to_rows(t + lo)
                    with pe.If(hi > lo):
                        to_rows(t + lo + 1, 1)
                        with pe.If(hi > lo + 1):
                            with pe.Fori(lo + 2, hi + 1) as k:
                                to_rows(t + k)
                    part_of_block(pe, begin, lo, times_wlin)
                    wait_turn(pe, "pe", s_max_lo, t + 1)
                    for h in range(H):
                        last = nc.tensor.transpose(ps_zT[:, h * P:(h + 1) * P], g[u][:, 0, h * P:(h + 1) * P], ident[:])
                    last.then_inc(s_zT_ps, 1)
                    for k in range(TOP):
                        wait_turn(pe, "pe", s_diag, t * TOP + (TOP + k + 1))
                        for h in range(H):
                            last = nc.tensor.matmul(ps_unit[:, h * P:(h + 1) * P], diag[:, k * H + h, :],
                                                    h_g[1 - u][:, k, :], start=(k == 0 and h == 0),
                                                    stop=(k == TOP - 1), skip_group_check=True)
                        if k == W_AFTER:
                            part_of_block(pe, begin, lo, times_w)
                        if k == FIRST_AFTER:
                            wait_turn(pe, "pe", s_zT, t + 1)
                            for h in range(H):
                                first = nc.tensor.matmul(ps_first[:, h:h + 1], z_T[:, h * P:(h + 1) * P],
                                                         a_T[:, h:h + 1], start=True, stop=True)
                            first.then_inc(s_first, 1)
                    last.then_inc(s_unit_ps, 1)
            wait_turn(pe, "pe", s_keys[0], n_pairs * 32 + 32)
            from_then_on(pe, whole_block)

        @block.vector
        def _(dve):
            V = nc.vector
            V.memset(x1_g[0][:], 0.0).then_inc(s_row_used, 1)
            V.memset(x1_g[1][:], 0.0).then_inc(s_max_hi, 1)
            V.memset(base[:], float(FIRST)).then_inc(s_prob, 1)
            V.memset(onehot[0][:], 0.0)
            V.memset(prob[:], 0.0).then_inc(s_score, 1)
            V.memset(score[:], 0.0).then_inc(s_h_g, 1)
            V.memset(linear[:], 0.0).then_inc(s_exp, 1)
            V.memset(n_unit[:], 0.0).then_inc(s_diag, TOP)

            dve.wait_ge(s_x, 32)
            V.tensor_reduce(row_sum[:], x_all[:], AX.X, ALU.add)
            dve.drain()
            V.tensor_scalar(mean[:], row_sum[:], 1.0 / D, None, ALU.mult)
            dve.drain()
            V.tensor_tensor(x_norm, x_all[:], mean[:, :, None].to_broadcast((P, NB, D)),
                            ALU.subtract).then_inc(s_stat, 1)
            dve.wait_ge(s_w, SETUP_W)
            dve.wait_ge(s_const, SETUP_CONST)
            V.tensor_tensor(unit_sum[:], w1_sb[:], a_sb[:], ALU.mult)
            dve.drain()
            V.tensor_reduce(w1a[:], unit_sum[:].rearrange("p (h o) -> p h o", h=H), AX.X, ALU.add)
            dve.drain()
            V.tensor_tensor(unit_sum[:], w2_sb[:], a_sb[:], ALU.mult)
            dve.drain()
            V.tensor_reduce(w2a[:], unit_sum[:].rearrange("p (h o) -> p h o", h=H), AX.X, ALU.add)
            V.tensor_scalar(a_sb[:], a_sb[:], 1.0 - SLOPE, None, ALU.mult)
            dve.drain()
            V.tensor_tensor(unit_sum[:].rearrange("p (h o) -> p h o", h=H), a_sb[:].rearrange("p (h o) -> p h o", h=H),
                            ident[:, None, :].to_broadcast((P, H, P)), ALU.mult)
            dve.drain()
            V.tensor_reduce(a_T[:], unit_sum[:].rearrange("p (h o) -> p h o", h=H), AX.X, ALU.add)
            dve.drain().then_inc(s_wa, 1)
            dve.wait_ge(s_sq, 1)
            V.tensor_reduce(var[:], x_sq, AX.X, ALU.add).then_inc(s_var, 1)
            dve.wait_ge(s_std, 1)
            V.reciprocal(rstd[:], std[:])
            dve.drain()
            V.tensor_tensor(x_norm, x_norm, rstd[:, :, None].to_broadcast((P, NB, D)), ALU.mult).then_inc(s_norm, 1)
            dve.drain()
            dve.wait_ge(s_const, SETUP_CONST)

            def search(v, between=None, meanwhile=None):
                for s in range(SEG):
                    V.max(c_val[:, s, :], adj_t[v][:, s:NP:SEG])
                    if between and s == SEG // 4:
                        between()
                dve.drain()
                for s in range(SEG):
                    V.max_index(c_idx[:, s, :], c_val[:, s, :], adj_t[v][:, s:NP:SEG])
                loaded = meanwhile() if meanwhile else None
                dve.drain()
                return loaded

            def count_units(n):
                V.scalar_tensor_tensor(c_col[:], c_idx[:].rearrange("p s e -> p (s e)"), float(SEG),
                                       seg_no[:].rearrange("p s e -> p (s e)"), ALU.mult, ALU.add)
                V.tensor_scalar(nonzero[:], c_val[:].rearrange("p s e -> p (s e)"), 0.0, 0.0, ALU.not_equal,
                                ALU.add, accum_out=n_cand[:])
                dve.drain()
                V.tensor_tensor(key[:], nonzero[:], c_col[:], ALU.mult)
                V.tensor_scalar(unit_flag[:], thresh[:], n_cand[:], 0.0, ALU.is_lt, ALU.add, accum_out=n_unit[:])
                V.scalar_tensor_tensor(far_pos[:], thresh[:], n_cand[:], far8[:], ALU.is_ge, ALU.mult)
                dve.drain()
                V.tensor_copy(n_unit16[:], n_unit[:]).then_inc(s_units, 1)

            def record_pair(m, q, n):
                if isinstance(q, int):
                    V.max(top[:, 0, :], key[:])
                    dve.drain()
                    V.match_replace(keys_left[:], top[:, 0, :], key[:], 0.0)
                else:
                    V.match_replace(keys_left[:], top[:, 1, :], keys_left[:], 0.0)
                    dve.drain()
                    V.max(top[:, 0, :], keys_left[:])
                    dve.drain()
                    V.match_replace(keys_left[:], top[:, 0, :], keys_left[:], 0.0)
                dve.drain()
                V.max(top[:, 1, :], keys_left[:])
                dve.drain()
                V.tensor_tensor(match[:, 0:TOP, :], top[:, 0, :, None].to_broadcast((P, TOP, CAND)),
                                key[:, None, :].to_broadcast((P, TOP, CAND)), ALU.is_equal).then_inc(s_match, 1)
                V.tensor_tensor(match[:, TOP:PAIR, :], top[:, 1, :, None].to_broadcast((P, TOP, CAND)),
                                key[:, None, :].to_broadcast((P, TOP, CAND)), ALU.is_equal)
                V.tensor_scalar(far_top[:], top[:], 0.0, FAR, ALU.is_equal, ALU.mult)
                dve.drain()
                V.tensor_tensor(match[:, TOP:PAIR, :], match[:, TOP:PAIR, :],
                                c_val[:].rearrange("p (z s) e -> p z (s e)", z=1).to_broadcast((P, TOP, CAND)), ALU.mult)
                wait_turn(dve, "dve", s_rec_left, m + 1)
                V.scalar_tensor_tensor(rec_out[:, :, R_COL:R_KEYF].bitcast(u32), far_top[:], -1.0, top[:],
                                       ALU.add, ALU.add)
                if isinstance(q, int):
                    wait_turn(dve, "dve", s_pos_ps, n + 1)
                    V.tensor_tensor(base_row[:], base[:], ps_pos[:, 0:1], ALU.add)
                    V.tensor_tensor(base[:], base[:], ps_pos[:, 1:2], ALU.add)
                    dve.drain()
                    V.scalar_tensor_tensor(pos_all[:], far_pos[:], base_row[:], rank_no[:], ALU.add, ALU.add)
                    V.scalar_tensor_tensor(pos[:], far_pos[:, 0:2], base_row[:], rank_no[:, 0:2], ALU.add, ALU.add)
                else:
                    dve.drain()
                    V.tensor_copy(pos[:], pos_all[:, bass.ds(q * 2, 2)])
                V.tensor_reduce(rec_out[:, 1, 0:TOP], match[:, TOP:PAIR, :], AX.X, ALU.add)
                wait_turn(dve, "dve", s_weighed, m + 1)
                V.tensor_reduce(rec_out[:, 0, 0:TOP], match[:, 0:TOP, :], AX.X, ALU.add)
                dve.drain().then_inc(s_scatter, 1)

            def more_pairs(n, m, per_batch):
                with dve.If(per_batch > 1):
                    with dve.Fori(1, per_batch) as q:
                        record_pair(m + q, q, n)

            def record_units(n, m, per_batch):
                count_units(n)
                record_pair(m, 0, n)
                more_pairs(n, m, per_batch)

            with dve.Fori(0, NB // 2) as i:
                for v in range(2):
                    b = i * 2 + v

                    def row_maxima():
                        wait_turn(dve, "dve", s_cnt, b + 1)
                        V.tensor_reduce(counts[v][:, C_SEG:C_SEG + 1], counts[v][:, 0:C_ROW], AX.X, ALU.max)
                        dve.drain()
                        V.scalar_tensor_tensor(count_max[v][:], counts[v][:, C_ROW:C_SEG + 1], 1.0, limits[:],
                                               ALU.max, ALU.min).then_inc(s_row_cnt, 1)

                    def load_range():
                        wait_turn(dve, "dve", s_cum, b + 1)
                        return (dve.value_load(cum[v][0:1, B_LO:B_LO + 1], min_val=0, max_val=CAP),
                                dve.value_load(cum[v][0:1, B_HI:B_HI + 1], min_val=1, max_val=CAP),
                                dve.value_load(cum[v][0:1, M_LO:M_LO + 1], min_val=0, max_val=CAP),
                                dve.value_load(cum[v][0:1, M_HI:M_HI + 1], min_val=1, max_val=CAP),
                                dve.value_load(cum[v][0:1, PER:PER + 1], min_val=1, max_val=RANKS // 2))

                    wait_turn(dve, "dve", s_adj[v], i * 16 + 16)
                    lo, hi, m_lo, m_hi, per_batch = search(v, row_maxima, load_range)
                    count_units(lo)
                    record_pair(m_lo, 0, lo)
                    with dve.If(m_hi - m_lo > 1):
                        more_pairs(lo, m_lo, per_batch)
                        with dve.If(hi - lo > 1):
                            with dve.Fori(1, hi - lo) as j:
                                for s in range(SEG):
                                    V.match_replace(adj_t[v][:, s:NP:SEG], c_val[:, s, :], adj_t[v][:, s:NP:SEG], TAKEN)
                                dve.drain()
                                search(v)
                                record_units(lo + j, dve.snap(m_lo + j * per_batch), per_batch)
                            V.memset(adj_t[v][:, N:NP], 0.0)
                    dve.drain().then_inc(s_adj_free, 1)
            V.tensor_scalar(n_list[:], base[0:1, :], float(-FIRST), None, ALU.add)
            dve.drain().then_inc(s_n_list, 1)

            dve.wait_ge(s_list, 1)
            n_pairs = tile_pairs(dve)

            def half(u, lo, hi, what):
                z = g[u][:, lo:hi, 0:HD]
                if what == "max":
                    return V.tensor_tensor(z, z, x1_g[u][:, None, 0:HD].to_broadcast((P, hi - lo, HD)), ALU.max)
                if what == "mult":
                    return V.tensor_tensor(z, z, a_sb[:, None, :].to_broadcast((P, hi - lo, HD)), ALU.mult)
                return V.tensor_reduce(score[:, lo:hi, :], z.rearrange("p s (h d) -> p s h d", h=H), AX.X, ALU.add)

            def mark_rows(k, z=0):
                V.scalar_tensor_tensor(onehot[z][:], col_no[:], block_row[:, bass.ds(k, 1)],
                                       row_key[u][:, 0:1].to_broadcast((P, P)), ALU.add, ALU.is_equal).then_inc(s_hot, 1)

            def add_rows(n, k, z=0):
                wait_turn(dve, "dve", s_row, n + 1)
                V.tensor_tensor(acc[:, k, :], acc[:, k, :], ps_row[z][:, 0:HD + H], ALU.add).then_inc(s_row_used, 1)

            def average(k, done):
                V.reciprocal(den_inv[:], acc[:, bass.ds(k, 1), HD:HD + H].rearrange("p z h -> p (z h)"))
                dve.drain()
                V.tensor_tensor(mean_h.rearrange("p (h d) -> p h d", h=H),
                                acc[:, bass.ds(k, 1), 0:HD].rearrange("p z (h d) -> p (z h) d", h=H),
                                den_inv[:, :, None].to_broadcast((P, H, D)), ALU.mult).then_inc(s_mean, 1)

            def leaky(k, done):
                wait_turn(dve, "dve", s_relu, done)
                V.scalar_tensor_tensor(leaky_T, ps_lin, SLOPE, relu_T, ALU.mult, ALU.add).then_inc(s_lin, 1)

            def result(k, done):
                wait_turn(dve, "dve", s_y_ps, done)
                wait_turn(dve, "dve", s_out, done * 16)
                V.tensor_tensor(y_t[:], ps_y, x_all[:, bass.ds(k, 1), :].rearrange("p z d -> p (z d)"),
                                ALU.add).then_inc(s_y, 1)

            def whole_block(k, done):
                average(k, done)
                leaky(k, done)
                result(k, done)

            with dve.Fori(0, n_pairs) as i:
                for u in range(2):
                    t = i * 2 + u
                    wait_turn(dve, "dve", s_g_lo[u], (i + 1) * (16 * (LO + 1)))
                    half(u, 0, LO, "max").then_inc(s_max_lo, 1)
                    wait_turn(dve, "dve", s_keys[u], i * 32 + 32)
                    begin, lo, hi = load_ends(dve, u, 3)
                    part_of_block(dve, begin, lo, average, others=whole_block)
                    wait_turn(dve, "dve", s_exp, t + 1)
                    wait_turn(dve, "dve", s_adj_w[1 - u], (i + 1) * 16)
                    wait_turn(dve, "dve", s_diag, t * TOP + TOP)
                    V.tensor_tensor(prob[:], e_exp[:].rearrange("p (s h) -> p s h", h=H),
                                    adj_w[1 - u][:, :, None].to_broadcast((P, TOP, H)), ALU.mult).then_inc(s_prob, 1)
                    dve.drain()
                    V.tensor_reduce(unit_den[1 - u][:], prob[:].rearrange("p s h -> p h s"), AX.X, ALU.add)
                    mark_rows(lo)
                    with dve.If(hi > lo):
                        mark_rows(next_block(lo), 1)
                    wait_turn(dve, "dve", s_g_hi[u], (i + 1) * (16 * (TOP - LO)))
                    half(u, LO, TOP, "max").then_inc(s_max_hi, 1)
                    V.tensor_tensor(linear[:], g[u][:, :, HD:XW], x1_g[u][:, None, HD:XW].to_broadcast((P, TOP, H)),
                                    ALU.add)
                    dve.drain()
                    half(u, LO, TOP, "mult")
                    add_rows(t + lo, lo)
                    with dve.If(hi > lo):
                        add_rows(t + lo + 1, next_block(lo), 1)
                        with dve.If(hi > lo + 1):
                            with dve.Fori(lo + 2, hi + 1) as k:
                                mark_rows(k)
                                add_rows(t + k, k)
                    dve.drain().then_inc(s_tile, 1)
                    half(u, LO, TOP, "sum")
                    part_of_block(dve, begin, lo, leaky)
                    wait_turn(dve, "dve", s_mul_lo, t + 1)
                    half(u, 1, LO, "sum")
                    dve.drain()
                    V.tensor_tensor(score[:, 1:TOP, :], score[:, 1:TOP, :], linear[:, 1:TOP, :], ALU.add)
                    wait_turn(dve, "dve", s_first, t + 1)
                    V.tensor_tensor(score[:, 0, :], ps_first, linear[:, 0, :], ALU.add).then_inc(s_score, 1)
                    part_of_block(dve, begin, lo, result)
            wait_turn(dve, "dve", s_g_lo[0], n_pairs * (16 * (LO + 1)) + 16 * (LO + 1))
            wait_turn(dve, "dve", s_g_hi[0], n_pairs * (16 * (TOP - LO)) + 16 * (TOP - LO))
            dve.drain()

            wait_turn(dve, "dve", s_keys[0], n_pairs * 32 + 32)
            from_then_on(dve, whole_block)


_INS = ["x", "adj", "L0_gnn_w1", "L0_gnn_w2", "L0_gnn_a", "L0_gnn_Wlin", "L0_gnn_w"]


def kernel(**inputs):
    import numpy as _np
    import concourse.bacc as _bacc
    from concourse import mybir as _mybir
    from concourse.bass_utils import run_bass_kernel_spmd as _run

    nc = _bacc.Bacc("TRN2", target_bir_lowering=False, num_devices=1)
    arrays, args = {}, []
    for name in _INS:
        arr = _np.ascontiguousarray(inputs[name])
        arrays[f"in_{name}"] = arr
        args.append(nc.dram_tensor(f"in_{name}", arr.shape, _mybir.dt.from_np(arr.dtype), kind="ExternalInput").ap())
    args.append(nc.dram_tensor("out_0", inputs["x"].shape, _mybir.dt.float32, kind="ExternalOutput").ap())
    gatv2_kernel(nc, *args)
    r = _run(nc, [arrays], core_ids=[0])
    return r.results[0]["out_0"]
```
